# Optimizing a Trainium2 kernel written in Bass

```python
import numpy as np
import jax
import jax.numpy as jnp

def _softmax(x, axis=-1):
    return jax.nn.softmax(x, axis=axis)
def _gelu(x):
    return jax.nn.gelu(x, approximate=True)
def _silu(x):
    return jax.nn.silu(x)
def _sigmoid(x):
    return jax.nn.sigmoid(x)
def _layernorm(x, axis=-1, eps=1e-5):
    m = jnp.mean(x, axis=axis, keepdims=True)
    v = jnp.var(x, axis=axis, keepdims=True)
    return (x - m) / jnp.sqrt(v + eps)
def _scatter_add(tgt, idx, src, axis=0):
    return tgt.at[idx].add(src)
def _segment_sum(src, seg, n):
    return jax.ops.segment_sum(src, seg, n)

kernel_name = 'mk_conv_seq_d1_conv_nchw512_4b6f95'

def setup_inputs(seed: int = 0):
    np.random.seed(seed)
    _w = jnp.asarray
    def _rec_inputs():
        import jax
        import jax.numpy as jnp
        _gk = jax.random.key(seed)
        x = -0.0003929 + 0.9999 * jax.random.normal(jax.random.fold_in(_gk, 1), (8, 512, 64, 64), jnp.float32)
        return x
    x = _rec_inputs()
    def _L0_conv_setup():
        import jax, jax.numpy as jnp
        import numpy as np
        LATENT_CH = 64

        def conv1x1(x, w):
            gain = 1.0 / np.sqrt(w.shape[1])
            return jnp.einsum('bchw,oc->bohw', x, w * gain)

        def casual_attention(q, k, v):
            score = jnp.einsum('bcn,bcm->bnm', q, k)
            score = jax.nn.softmax(score, axis=-1)
            return jnp.einsum('bnm,bcm->bnc', score, v)
        key = jax.random.key(seed)
        ks = jax.random.split(key, 8)
        B, C, H, W = (8, 512, 64, 64)
        L, P = (LATENT_CH, 256)
        return {'feature_map': jax.random.normal(ks[0], (B, C, H, W), jnp.float32), 'concepts': jax.random.normal(ks[1], (P, L), jnp.float32), 'w_theta': jax.random.normal(ks[2], (L, C), jnp.float32), 'w_phi': jax.random.normal(ks[3], (L, C), jnp.float32), 'w_g': jax.random.normal(ks[4], (L, C), jnp.float32), 'w_o': jax.random.normal(ks[5], (C, L), jnp.float32), 'gamma_sa': jnp.float32(0.1), 'gamma_moca': jnp.float32(0.1)}
    _L0_conv_all = _L0_conv_setup()
    _L0_conv_in = {k: v for k, v in _L0_conv_all.items() if k in ('concepts', 'w_theta', 'w_phi', 'w_g', 'w_o', 'gamma_sa', 'gamma_moca', )}
    del _L0_conv_all

    return {
        "x": x,
        "L0_conv_concepts": _L0_conv_in["concepts"],
        "L0_conv_w_theta": _L0_conv_in["w_theta"],
        "L0_conv_w_phi": _L0_conv_in["w_phi"],
        "L0_conv_w_g": _L0_conv_in["w_g"],
        "L0_conv_w_o": _L0_conv_in["w_o"],
        "L0_conv_gamma_sa": _L0_conv_in["gamma_sa"],
        "L0_conv_gamma_moca": _L0_conv_in["gamma_moca"],
    }

def reference(x, L0_conv_concepts, L0_conv_w_theta, L0_conv_w_phi, L0_conv_w_g, L0_conv_w_o, L0_conv_gamma_sa, L0_conv_gamma_moca):
    import jax
    import jax.numpy as jnp
    def _L0_conv_ref(feature_map, concepts, w_theta, w_phi, w_g, w_o, gamma_sa, gamma_moca):
        import jax, jax.numpy as jnp
        import numpy as np
        LATENT_CH = 64

        def conv1x1(x, w):
            gain = 1.0 / np.sqrt(w.shape[1])
            return jnp.einsum('bchw,oc->bohw', x, w * gain)

        def casual_attention(q, k, v):
            score = jnp.einsum('bcn,bcm->bnm', q, k)
            score = jax.nn.softmax(score, axis=-1)
            return jnp.einsum('bnm,bcm->bnc', score, v)
        B, C, H, W = feature_map.shape
        L = LATENT_CH
        HW = H * W
        th = conv1x1(feature_map, w_theta).reshape(B, L, HW)
        ph = conv1x1(feature_map, w_phi).reshape(B, L, HW)
        g = conv1x1(feature_map, w_g).reshape(B, L, HW)
        lat = casual_attention(th, ph, g).reshape(B, L, H, W)
        sa_out = gamma_sa * conv1x1(lat, w_o) + feature_map
        enc = conv1x1(sa_out, w_theta).reshape(B, L, HW)
        phi_c = concepts.T[None]
        phi_c = jnp.broadcast_to(phi_c, (B, L, concepts.shape[0]))
        lat2 = casual_attention(enc, phi_c, phi_c).reshape(B, L, H, W)
        out = gamma_moca * conv1x1(lat2, w_o) + sa_out
        return out

    def _gn(v, G=32, eps=1e-5):
        B_, C_, H_, W_ = v.shape
        g = v.reshape(B_, G, C_ // G, H_, W_)
        m = jnp.mean(g, axis=(2, 3, 4), keepdims=True)
        s = jnp.var(g, axis=(2, 3, 4), keepdims=True)
        return ((g - m) / jnp.sqrt(s + eps)).reshape(v.shape)

    def _ln_c(v, eps=1e-6):
        m = jnp.mean(v, axis=1, keepdims=True)
        s = jnp.var(v, axis=1, keepdims=True)
        return (v - m) / jnp.sqrt(s + eps)

    def _ln_t(v, eps=1e-5):
        m = jnp.mean(v, axis=-1, keepdims=True)
        s = jnp.var(v, axis=-1, keepdims=True)
        return (v - m) / jnp.sqrt(s + eps)

    def _to_tokens(v):
        B_, C_, H_, W_ = v.shape
        return v.reshape(B_, C_, H_ * W_).transpose(0, 2, 1)
    def _from_tokens(t, like):
        B_, C_, H_, W_ = like.shape
        return t.transpose(0, 2, 1).reshape(B_, C_, H_, W_)

    x = _L0_conv_ref(x, L0_conv_concepts, L0_conv_w_theta, L0_conv_w_phi, L0_conv_w_g, L0_conv_w_o, L0_conv_gamma_sa, L0_conv_gamma_moca)
    return x


_drawn_inputs = setup_inputs


def setup_inputs(seed=0):
    import zlib

    import numpy as np

    out = dict(_drawn_inputs(seed))
    spreads = {}
    factors = {}
    for name, (base, spread) in spreads.items():
        noise = np.random.default_rng([zlib.crc32(name.encode()), seed]).standard_normal(out[name].shape)
        drawn = base * np.exp(spread * noise) if base else spread * noise
        out[name] = jnp.asarray(drawn.astype(out[name].dtype))
    for name, factor in factors.items():
        out[name] = (out[name] * factor).astype(out[name].dtype)
    return out
```

```python
import math

import concourse.bass as bass
from concourse import mybir
from contextlib import ExitStack

BATCH, CH, LATENT, CONCEPTS = 8, 512, 64, 256
PIXELS = 64 * 64
PART = 128
BLOCK = 512
BLOCKS = PIXELS // BLOCK
SUBS = BLOCK // PART
KTILES = CH // PART
KEYTILES = PIXELS // PART
CTILES = CONCEPTS // PART
XSLOTS = 4
NE = 4

MAXES = BLOCKS * SUBS
ENTRIES = MAXES + 1
SHIFT_STEP = 27
SETUP_STEPS = 6
SEARCHED = [min(MAXES, -(-(t + 1) * MAXES // 25)) for t in range(KEYTILES)]


def attention_kernel(nc, x, w_thetaphi, w_g, w_o_t, w_o, concepts_t, concepts, gamma_sa, gamma_moca, consts, out):
    fp32 = mybir.dt.float32
    fp32r = mybir.dt.float32r
    ALU = mybir.AluOpType
    ACT = mybir.ActivationFunctionType
    AX = mybir.AxisListType
    ds = bass.ds

    x_view = x.rearrange("b (k p) n -> b p k n", p=PART)
    out_view = out.rearrange("b (k p) n -> b p k n", p=PART)
    lat_dram = nc.dram_tensor("lat_scratch", (BATCH, PIXELS * LATENT), fp32).ap()
    clat_dram = nc.dram_tensor("clat_scratch", (BATCH, PIXELS * LATENT), fp32).ap()
    lat_store = lat_dram.rearrange("b (j s p c) -> b j p s c", j=BLOCKS, s=SUBS, p=PART)
    clat_store = clat_dram.rearrange("b (j s p c) -> b j p s c", j=BLOCKS, s=SUBS, p=PART)
    lat_load = lat_dram.rearrange("b (l n) -> b l n", l=LATENT)
    clat_load = clat_dram.rearrange("b (l n) -> b l n", l=LATENT)

    ctx = ExitStack()
    with ctx:
        def sb(name, shape, dt=fp32):
            return ctx.enter_context(nc.sbuf_tensor(name, shape, dt))

        def bank(name, shape=(PART, 512)):
            return ctx.enter_context(nc.psum_tensor(name, list(shape), fp32))

        def sem(name):
            return ctx.enter_context(nc.semaphore(name))

        ident = sb("ident", [PART, PART])
        neg_ident = sb("neg_ident", [PART, PART], fp32r)
        two_ident = sb("two_ident", [PART, LATENT], fp32r)
        raw_tp = sb("raw_tp", [PART, KTILES, PART])
        raw_g = sb("raw_g", [PART, KTILES, LATENT])
        raw_o = sb("raw_o", [PART, KTILES, LATENT])
        raw_ot = sb("raw_ot", [PART, CH])
        raw_ct = sb("raw_ct", [PART, CONCEPTS])
        gamma = sb("gamma", [PART, 2])
        w_tp = sb("w_tp", [PART, KTILES, PART])
        w_gs = sb("w_gs", [PART, KTILES, LATENT])
        w_os = sb("w_os", [PART, KTILES, LATENT])
        w_ot_high = sb("w_ot_high", [PART, CH], fp32r)
        w_ot_low = sb("w_ot_low", [PART, CH], fp32r)
        w_to_sum = sb("w_to_sum", [LATENT, LATENT])
        w_to_high = sb("w_to_high", [PART, LATENT], fp32r)
        w_to_low = sb("w_to_low", [PART, LATENT], fp32r)
        ckeys_high = sb("ckeys_high", [PART, CONCEPTS], fp32r)
        ckeys_low = sb("ckeys_low", [PART, CONCEPTS], fp32r)
        cvalues = sb("cvalues", [PART, CTILES, LATENT + 1])

        x_in = sb("x_in", [PART, XSLOTS, KTILES, BLOCK])
        queries = sb("queries", [PART, 2, PIXELS], fp32r)
        queries_shift = sb("queries_shift", [PART, PIXELS], fp32r)
        keys_high = sb("keys_high", [PART, PIXELS], fp32r)
        keys_low = sb("keys_low", [PART, PIXELS], fp32r)
        values = sb("values", [PART, KEYTILES, LATENT + 1])
        search_q = sb("search_q", [PART, 2, BLOCK], fp32r)
        tile_max = sb("tile_max", [PART, SUBS, BLOCKS])
        row_max = sb("row_max", [PART, SUBS], fp32r)
        probs = sb("probs", [PART, NE, BLOCK])
        sums_t = sb("sums_t", [LATENT + 1, BLOCK])
        inv = sb("inv", [PART, SUBS])
        lat_out = sb("lat_out", [PART, SUBS, LATENT])

        lat_in = sb("lat_in", [PART, BLOCK])
        lat_split = sb("lat_split", [PART, BLOCK], fp32r)
        cqueries = sb("cqueries", [PART, BLOCK], fp32r)
        cqueries_shift = sb("cqueries_shift", [PART, BLOCK], fp32r)
        crow_max = sb("crow_max", [PART, SUBS], fp32r)
        cprobs = sb("cprobs", [PART, CTILES, BLOCK])
        csums_t = sb("csums_t", [LATENT + 1, BLOCK])
        cinv = sb("cinv", [PART, SUBS])
        clat_out = sb("clat_out", [PART, SUBS, LATENT])

        mix_in = sb("mix_in", [PART, 2, BLOCK])
        mix = sb("mix", [PART, BLOCK])
        mix_split = sb("mix_split", [PART, BLOCK], fp32r)
        resid = sb("resid", [PART, KTILES, BLOCK])

        score_bank = [bank(f"score_bank{i}") for i in range(2)]
        max_bank = [bank(f"max_bank{i}") for i in range(2)]
        sum_bank = [bank(f"sum_bank{i}") for i in range(2)]
        side_bank = [bank(f"side_bank{i}") for i in range(2)]

        consts_in, weights_in = sem("consts_in"), sem("weights_in")
        x_loaded = [sem(f"x_loaded{i}") for i in range(XSLOTS)]
        search_q_loaded = [sem(f"search_q_loaded{i}") for i in range(2)]
        lat_stored, clat_stored, out_stored = sem("lat_stored"), sem("clat_stored"), sem("out_stored")
        lat_loaded, mix_loaded, resid_loaded = sem("lat_loaded"), sem("mix_loaded"), sem("resid_loaded")
        setup_dve, setup_pe, setup_ready = sem("setup_dve"), sem("setup_pe"), sem("setup_ready")
        thetaphi_ready, values_ready = sem("thetaphi_ready"), sem("values_ready")
        high_ready, low_ready, values_copied = sem("high_ready"), sem("low_ready"), sem("values_copied")
        max_ready, max_taken = sem("max_ready"), sem("max_taken")
        row_max_ready = sem("row_max_ready")
        scores_ready, probs_ready, probs_used = sem("scores_ready"), sem("probs_ready"), sem("probs_used")
        sums_copied, sums_turned = sem("sums_copied"), sem("sums_turned")
        inv_ready, lat_ready = sem("inv_ready"), sem("lat_ready")
        lat_high, lat_low = sem("lat_high"), sem("lat_low")
        enc_ready, enc_high, enc_low = sem("enc_ready"), sem("enc_high"), sem("enc_low")
        cmax_ready, crow_max_ready = sem("cmax_ready"), sem("crow_max_ready")
        cshift_ready, cshift_taken = sem("cshift_ready"), sem("cshift_taken")
        cscores_ready, cprobs_ready = sem("cscores_ready"), sem("cprobs_ready")
        csums_ready, csums_copied, csums_turned = sem("csums_ready"), sem("csums_copied"), sem("csums_turned")
        cinv_ready, clat_ready = sem("cinv_ready"), sem("clat_ready")
        mix_added, mix_high, mix_low = sem("mix_added"), sem("mix_high"), sem("mix_low")
        resid_ready, resid_added = sem("resid_ready"), sem("resid_added")

        raw = lambda ap: ap.bitcast(fp32)

        def block_cols(j):
            return ds(j * BLOCK, BLOCK) if not isinstance(j, int) else slice(j * BLOCK, (j + 1) * BLOCK)

        def q_cols(b, j):
            at = (b % 2) * PIXELS + j * BLOCK
            return ds(at, BLOCK) if not isinstance(at, int) else slice(at, at + BLOCK)

        queries_flat = queries[:, :, :].rearrange("p a n -> p (a n)")

        def schedule(loop, project, attend, finish, tail):
            def batch(b, side):
                project(b)
                attend(b, 0, 0, side, first=True)
                with loop(0, (BLOCKS - 2) // 2) as pair:
                    attend(b, 2 * pair + 1, 1, side)
                    attend(b, 2 * pair + 2, 0, side)
                attend(b, BLOCKS - 1, 1, side, last=True)
                finish(b)

            batch(0, 0)
            batch(1, 1)
            with loop(2, BATCH - 1) as b:
                batch(b, 2)
            batch(BATCH - 1, 2)
            with loop(0, BLOCKS) as j:
                tail(j, True)
            with loop(0, BLOCKS) as j:
                tail(j, False)

        block = ctx.enter_context(nc.Block())

        @block.sync
        def _(sp):
            sp.dma_start(ident[:, :], consts).then_inc(consts_in, 16)
            for dst, src in ((raw_tp[:, :, :], w_thetaphi), (raw_g[:, :, :], w_g), (raw_o[:, :, :], w_o),
                             (cvalues[:, :, 0:LATENT], concepts),
                             (raw_ot[0:64, :], w_o_t), (raw_ot[64:128, :], w_o_t),
                             (raw_ct[0:64, :], concepts_t), (raw_ct[64:128, :], concepts_t),
                             (gamma[:, 0:1], gamma_sa.partition_broadcast(PART)),
                             (gamma[:, 1:2], gamma_moca.partition_broadcast(PART))):
                sp.dma_start(dst, src).then_inc(weights_in, 16)

            def load_x(b, j, slot):
                src = x_view[ds(b, 1), :, :, block_cols(j)].rearrange("a p k n -> (a p) k n")
                sp.dma_start(x_in[:, slot, :, :], src).then_inc(x_loaded[slot], 16)

            for u in range(XSLOTS):
                load_x(0, u, u)

            def load_search_q(b, j, parity):
                sp.dma_start(raw(search_q[:, parity, :]), raw(queries_flat[:, q_cols(b, j)]))\
                  .then_inc(search_q_loaded[parity], 16)

            def project(b):
                for u in range(XSLOTS):
                    sp.wait_ge(values_ready, b * BLOCKS + u + 1)
                    load_x(b, XSLOTS + u, u)
                    if u < 2:
                        sp.wait_ge(low_ready, b * BLOCKS + u + 1)
                        load_search_q(b, u, u)

            def load_next(b, j):
                sp.wait_ge(max_ready, (b * BLOCKS + j + 1) * ENTRIES)
                load_search_q(b, j + 2, j % 2)

            def counted(value):
                return value if isinstance(value, int) else sp.snap(value)

            def load_side(b, j, side):
                n1 = counted((b - 1) * BLOCKS + j)
                n2 = counted((b - 2) * BLOCKS + j)
                if side >= 1:
                    sp.wait_ge(lat_stored, 16 * BLOCKS * b)
                    sp.wait_ge(lat_low, n1)
                    src = lat_load[ds(b - 1, 1), :, block_cols(j)].rearrange("a l n -> (a l) n")
                    sp.dma_start(lat_in[0:64, :], src).then_inc(lat_loaded, 16)
                    sp.dma_start(lat_in[64:128, :], src).then_inc(lat_loaded, 16)
                if side >= 2:
                    load_output(b - 2, j, n2)

            def load_output(b2, j, n2):
                sp.wait_ge(clat_stored, 16 * BLOCKS * (b2 + 1))
                sp.wait_ge(mix_added, n2)
                for half in (0, 64):
                    for i, view in enumerate((lat_load, clat_load)):
                        src = view[ds(b2, 1), :, block_cols(j)].rearrange("a l n -> (a l) n")
                        sp.dma_start(mix_in[half:half + 64, i, :], src).then_inc(mix_loaded, 16)
                sp.wait_ge(out_stored, 16 * n2)
                src = x_view[ds(b2, 1), :, :, block_cols(j)].rearrange("a p k n -> (a p) k n")
                sp.dma_start(resid[:, :, :], src).then_inc(resid_loaded, 16)

            def store_lat(b, j):
                sp.wait_ge(lat_ready, b * BLOCKS + j + 1)
                dst = lat_store[ds(b, 1), ds(j, 1), :, :, :].rearrange("a j p s c -> (a j p) s c")
                sp.dma_start(dst, lat_out[:, :, :]).then_inc(lat_stored, 16)

            def store_clat(b1, j):
                sp.wait_ge(clat_ready, b1 * BLOCKS + j + 1)
                dst = clat_store[ds(b1, 1), ds(j, 1), :, :, :].rearrange("a j p s c -> (a j p) s c")
                sp.dma_start(dst, clat_out[:, :, :]).then_inc(clat_stored, 16)

            def store_out(b2, j):
                sp.wait_ge(resid_added, KTILES * (b2 * BLOCKS + j + 1))
                dst = out_view[ds(b2, 1), :, :, block_cols(j)].rearrange("a p k n -> (a p) k n")
                sp.dma_start(dst, resid[:, :, :]).then_inc(out_stored, 16)

            def attend(b, j, side):
                load_side(b, j, side)
                if j < BLOCKS - 2:
                    load_next(b, j)
                if j == 0 and not (isinstance(b, int) and b == BATCH - 1):
                    sp.wait_ge(values_ready, (b + 1) * BLOCKS)
                    for u in range(XSLOTS):
                        load_x(b + 1, u, u)
                if j > 0:
                    store_lat(b, j - 1)
                if side >= 1:
                    store_clat(b - 1, j)
                if side >= 2:
                    store_out(b - 2, j)

            def tail(j, concept):
                if concept:
                    load_side(BATCH, j, 2)
                    store_clat(BATCH - 1, j)
                    store_out(BATCH - 2, j)
                else:
                    load_output(BATCH - 1, j, counted((BATCH - 1) * BLOCKS + j))
                    store_out(BATCH - 1, j)

            def batch(b, side):
                project(b)
                for j in range(BLOCKS):
                    attend(b, j, side)
                store_lat(b, BLOCKS - 1)

            batch(0, 0)
            batch(1, 1)
            with sp.Fori(2, BATCH - 1) as b:
                batch(b, 2)
            batch(BATCH - 1, 2)
            with sp.Fori(0, BLOCKS) as j:
                tail(j, True)
            with sp.Fori(0, BLOCKS) as j:
                tail(j, False)

            sp.wait_ge(lat_stored, 16 * BATCH * BLOCKS)
            sp.wait_ge(clat_stored, 16 * BATCH * BLOCKS)
            sp.wait_ge(out_stored, 16 * BATCH * BLOCKS)

        @block.scalar
        def _(act):
            def project(b):
                with act.Fori(0, BLOCKS // 2) as pair:
                    for parity in range(2):
                        j = 2 * pair + parity
                        kb = b * BLOCKS + j
                        tp = score_bank[parity]
                        act.wait_ge(thetaphi_ready, kb + 1)
                        nc.scalar.activation(queries_flat[0:64, q_cols(b, j)], tp[0:64, :], ACT.Copy)
                        nc.scalar.activation(keys_high[0:64, block_cols(j)], tp[64:128, :], ACT.Copy)
                        nc.scalar.activation(keys_high[64:128, block_cols(j)], tp[64:128, :], ACT.Copy)
                        nc.scalar.activation(queries_shift[0:64, block_cols(j)], tp[0:64, :], ACT.Copy)\
                            .then_inc(high_ready, 1)
                        act.wait_ge(values_ready, kb + 1)
                        nc.scalar.activation(values[:, ds(j * SUBS, SUBS), 0:LATENT],
                                             side_bank[parity][:, 0:SUBS * LATENT].rearrange("p (s c) -> p s c", s=SUBS),
                                             ACT.Copy).then_inc(values_copied, 1)

            def copy_sums(b, j, parity):
                kb = b * BLOCKS + j
                act.wait_ge(probs_used, (kb + 1) * KEYTILES)
                act.wait_ge(sums_turned, kb)
                nc.scalar.activation(sums_t[:, :], sum_bank[parity][0:LATENT + 1, :], ACT.Copy)\
                    .then_inc(sums_copied, 1)

            def exp_scores(b, j, t):
                n = (b * BLOCKS + j) * KEYTILES + t
                act.wait_ge(scores_ready, n + 1)
                if not (isinstance(n, int) and n < NE):
                    act.wait_ge(probs_used, n - NE + 1)
                nc.scalar.activation(probs[:, t % NE, :], score_bank[t % 2][:, :], ACT.Exp)\
                    .then_inc(probs_ready, 1)

            def concept_step(step, n1):
                if step == "lat":
                    act.wait_ge(lat_loaded, 32 * (n1 + 1))
                    act.wait_ge(enc_ready, n1)
                    nc.scalar.activation(lat_split[:, :], lat_in[:, :], ACT.Copy).then_inc(lat_high, 1)
                if step == "enc":
                    act.wait_ge(enc_ready, n1 + 1)
                    nc.scalar.activation(cqueries[0:64, :], side_bank[0][0:64, :], ACT.Copy)
                    nc.scalar.activation(cqueries_shift[0:64, :], side_bank[0][0:64, :], ACT.Copy)\
                        .then_inc(enc_high, 1)
                if step == "probs":
                    for t in range(CTILES):
                        act.wait_ge(cscores_ready, CTILES * n1 + t + 1)
                        nc.scalar.activation(cprobs[:, t, :], side_bank[1 - t][:, :], ACT.Exp)\
                            .then_inc(cprobs_ready, 1)
                if step == "sums":
                    act.wait_ge(csums_ready, n1 + 1)
                    nc.scalar.activation(csums_t[:, :], side_bank[1][0:LATENT + 1, :], ACT.Copy)\
                        .then_inc(csums_copied, 1)

            def output_step(n2):
                act.wait_ge(mix_added, n2 + 1)
                nc.scalar.activation(mix_split[:, :], mix[:, :], ACT.Copy).then_inc(mix_high, 1)

            def attend(b, j, parity, side, first=False, last=False):
                n = b * BLOCKS + j
                for t in range(KEYTILES):
                    if t == 1 and not first:
                        copy_sums(b, j - 1, 1 - parity)
                    exp_scores(b, j, t)
                    if side >= 1 and t in ACT_CONCEPT:
                        concept_step(ACT_CONCEPT[t], n - BLOCKS)
                    if side >= 2 and t == ACT_OUTPUT:
                        output_step(n - 2 * BLOCKS)

            def tail(j, concept):
                if concept:
                    for step in ("lat", "enc", "probs", "sums"):
                        concept_step(step, (BATCH - 1) * BLOCKS + j)
                    output_step((BATCH - 2) * BLOCKS + j)
                else:
                    output_step((BATCH - 1) * BLOCKS + j)

            schedule(act.Fori, project, attend, lambda b: copy_sums(b, BLOCKS - 1, 1), tail)

        @block.vector
        def _(dve):
            steps = [0]

            def then(ins):
                steps[0] += 1
                ins.then_inc(setup_dve, 1)
                dve.wait_ge(setup_dve, steps[0])

            gain = float(1.0 / math.sqrt(CH))
            out_gain = float(1.0 / math.sqrt(LATENT))
            nc.vector.memset(raw(keys_low[64:128, :]), 0.0)
            nc.vector.memset(raw(queries_shift[64:128, :]), 0.0)
            nc.vector.memset(raw(ckeys_low[64:128, :]), 0.0)
            nc.vector.memset(raw(cqueries_shift[64:128, :]), 0.0)
            nc.vector.memset(values[:, :, LATENT:LATENT + 1], 1.0)
            then(nc.vector.memset(cvalues[:, :, LATENT:LATENT + 1], 1.0))
            nc.vector.memset(raw(keys_low[64:65, :]), 1.0)
            then(nc.vector.memset(raw(ckeys_low[64:65, :]), 1.0))
            dve.wait_ge(consts_in, 16)
            nc.vector.tensor_scalar(neg_ident[:, :], ident[:, :], -1.0, None, ALU.mult)
            nc.vector.tensor_copy(two_ident[0:64, :], ident[0:64, 0:64])
            nc.vector.tensor_copy(two_ident[64:128, :], ident[64:128, 64:128])
            dve.wait_ge(weights_in, 16 * 10)
            nc.vector.tensor_scalar(w_tp[:, :, :], raw_tp[:, :, :], gain, None, ALU.mult)
            then(nc.vector.tensor_scalar(raw_g[:, :, :], raw_g[:, :, :], gain, None, ALU.mult))
            nc.vector.tensor_scalar(w_gs[:, :, :], raw_g[:, :, :], gamma[:, 0:1], None, ALU.mult)
            nc.vector.tensor_scalar(w_os[:, :, :], raw_o[:, :, :], out_gain, None, ALU.mult)
            nc.vector.tensor_scalar(raw_ot[:, :], raw_ot[:, :], out_gain, None, ALU.mult)
            nc.vector.tensor_scalar(cvalues[:, :, 0:LATENT], cvalues[:, :, 0:LATENT], gamma[:, 1:2], None, ALU.mult)
            nc.vector.tensor_copy(ckeys_high[:, :], raw_ct[:, :])
            then(nc.vector.memset(tile_max[:, :, :], 0.0))
            then(nc.vector.tensor_copy(w_ot_high[:, :], raw_ot[:, :]))
            nc.vector.tensor_tensor(w_ot_low[:, :], raw_ot[:, :], raw(w_ot_high[:, :]), ALU.subtract)
            then(nc.vector.tensor_tensor(ckeys_low[0:64, :], raw_ct[0:64, :], raw(ckeys_high[0:64, :]), ALU.subtract))
            assert steps[0] == SETUP_STEPS
            dve.wait_ge(setup_pe, 1)
            nc.vector.tensor_copy(w_to_high[0:64, :], side_bank[0][0:64, 0:LATENT])
            then(nc.vector.tensor_copy(w_to_high[64:128, :], side_bank[0][0:64, 0:LATENT]))
            nc.vector.tensor_tensor(w_to_low[0:64, :], side_bank[0][0:64, 0:LATENT],
                                    raw(w_to_high[0:64, :]), ALU.subtract)
            nc.vector.tensor_tensor(w_to_low[64:128, :], side_bank[0][0:64, 0:LATENT],
                                    raw(w_to_high[0:64, :]), ALU.subtract).then_inc(setup_ready, 1)

            def take_max(b, j, parity, i):
                dve.wait_ge(max_ready, (b * BLOCKS + j) * ENTRIES + i + 1)
                nc.vector.reduce_max(tile_max[:, i % SUBS, i // SUBS:i // SUBS + 1],
                                     max_bank[(parity + i) % 2][:, :], AX.X).then_inc(max_taken, 1)

            def finish_max(b, j, parity):
                kb = b * BLOCKS + j
                dve.wait_ge(max_taken, kb * ENTRIES + MAXES)
                nc.vector.tensor_reduce(row_max[:, :], tile_max[:, :, :], AX.X, ALU.max).then_inc(row_max_ready, 1)
                dve.wait_ge(max_ready, (kb + 1) * ENTRIES)
                nc.vector.tensor_copy(queries_shift[64:65, block_cols(j)],
                                      max_bank[(parity + MAXES) % 2][0:1, :]).then_inc(max_taken, 1)

            def project(b):
                with dve.Fori(0, BLOCKS // 2) as pair:
                    for parity in range(2):
                        j = 2 * pair + parity
                        kb = b * BLOCKS + j
                        tp = score_bank[parity]
                        dve.wait_ge(high_ready, kb + 1)
                        nc.vector.tensor_tensor(queries_flat[64:128, q_cols(b, j)], tp[0:64, :],
                                                raw(queries_flat[0:64, q_cols(b, j)]), ALU.subtract)
                        nc.vector.tensor_tensor(keys_low[0:64, block_cols(j)], tp[64:128, :],
                                                raw(keys_high[64:128, block_cols(j)]), ALU.subtract)\
                            .then_inc(low_ready, 1)
                        for s in range(SUBS):
                            dve.wait_ge(max_ready, b * BLOCKS * ENTRIES + j * SUBS + s + 1)
                            nc.vector.reduce_max(tile_max[:, s, ds(j, 1)], max_bank[s % 2][:, :], AX.X)\
                                .then_inc(max_taken, 1)
                finish_max(b, 0, 0)

            def normalize(b, j):
                kb = b * BLOCKS + j
                turned = side_bank[1][:, 0:SUBS * (LATENT + 1)].rearrange("p (s c) -> p s c", s=SUBS)
                dve.wait_ge(sums_turned, kb + 1)
                nc.vector.reciprocal(inv[:, :], turned[:, :, LATENT]).then_inc(inv_ready, 1)
                dve.wait_ge(inv_ready, kb + 1)
                dve.wait_ge(lat_stored, 16 * kb)
                nc.vector.tensor_tensor(lat_out[:, :, :], turned[:, :, 0:LATENT],
                                        inv[:, :].unsqueeze(2).to_broadcast([PART, SUBS, LATENT]), ALU.mult)\
                    .then_inc(lat_ready, 1)

            def concept_step(step, n1):
                if step == "lat":
                    dve.wait_ge(lat_high, n1 + 1)
                    nc.vector.tensor_tensor(lat_split[64:128, :], lat_in[64:128, :], raw(lat_split[64:128, :]),
                                            ALU.subtract).then_inc(lat_low, 1)
                if step == "enc":
                    dve.wait_ge(enc_high, n1 + 1)
                    nc.vector.tensor_tensor(cqueries[64:128, :], side_bank[0][0:64, :], raw(cqueries[0:64, :]),
                                            ALU.subtract).then_inc(enc_low, 1)
                if step == "max":
                    for i in range(2):
                        dve.wait_ge(cmax_ready, 2 * n1 + i + 1)
                        nc.vector.tensor_reduce(crow_max[:, 2 * i:2 * i + 2],
                                                side_bank[i][:, :].rearrange("p (s m) -> p s m", s=2),
                                                AX.X, ALU.max).then_inc(crow_max_ready, 1)
                if step == "shift":
                    dve.wait_ge(cshift_ready, n1 + 1)
                    nc.vector.tensor_copy(cqueries_shift[64:65, :], side_bank[0][0:1, :]).then_inc(cshift_taken, 1)
                if step == "normalize":
                    turned = side_bank[0][:, 0:SUBS * (LATENT + 1)].rearrange("p (s c) -> p s c", s=SUBS)
                    dve.wait_ge(csums_turned, n1 + 1)
                    nc.vector.reciprocal(cinv[:, :], turned[:, :, LATENT]).then_inc(cinv_ready, 1)
                    dve.wait_ge(cinv_ready, n1 + 1)
                    dve.wait_ge(clat_stored, 16 * n1)
                    nc.vector.tensor_tensor(clat_out[:, :, :], turned[:, :, 0:LATENT],
                                            cinv[:, :].unsqueeze(2).to_broadcast([PART, SUBS, LATENT]), ALU.mult)\
                        .then_inc(clat_ready, 1)

            def output_step(step, n2):
                if step == "mix":
                    dve.wait_ge(mix_loaded, 64 * (n2 + 1))
                    nc.vector.tensor_tensor(mix[:, :], mix_in[:, 0, :], mix_in[:, 1, :], ALU.add)\
                        .then_inc(mix_added, 1)
                if step == "low":
                    dve.wait_ge(mix_high, n2 + 1)
                    nc.vector.tensor_tensor(mix_split[64:128, :], mix[64:128, :], raw(mix_split[64:128, :]),
                                            ALU.subtract).then_inc(mix_low, 1)
                if step in (0, 2):
                    for k in (step, step + 1):
                        if k == 0:
                            dve.wait_ge(resid_loaded, 16 * (n2 + 1))
                        dve.wait_ge(resid_ready, KTILES * n2 + k + 1)
                        nc.vector.tensor_tensor(resid[:, k, :], resid[:, k, :], side_bank[1 - k % 2][:, :], ALU.add)\
                            .then_inc(resid_added, 1)

            def attend(b, j, parity, side, first=False, last=False):
                n = b * BLOCKS + j
                done = 0
                for t in range(KEYTILES):
                    if not last:
                        for i in range(done, SEARCHED[t]):
                            take_max(b, j + 1, 1 - parity, i)
                        done = SEARCHED[t]
                        if t == SHIFT_STEP:
                            finish_max(b, j + 1, 1 - parity)
                    if t == TURN_STEP and not first:
                        normalize(b, j - 1)
                    if side >= 1 and t in DVE_CONCEPT:
                        concept_step(DVE_CONCEPT[t], n - BLOCKS)
                    if side >= 2 and t in DVE_OUTPUT:
                        output_step(DVE_OUTPUT[t], n - 2 * BLOCKS)

            def tail(j, concept):
                if concept:
                    for step in ("lat", "enc", "max", "shift", "normalize"):
                        concept_step(step, (BATCH - 1) * BLOCKS + j)
                for step in ("mix", "low", 0, 2):
                    output_step(step, (BATCH - 2 if concept else BATCH - 1) * BLOCKS + j)

            schedule(dve.Fori, project, attend, lambda b: normalize(b, BLOCKS - 1), tail)

        @block.tensor
        def _(pe):
            mm = nc.tensor.matmul
            pe.wait_ge(setup_dve, SETUP_STEPS)
            for k in range(KTILES):
                last = mm(side_bank[0][0:64, 0:LATENT], w_os[:, k, :], w_tp[:, k, 0:LATENT],
                          start=k == 0, stop=k == KTILES - 1)
            last.then_inc(setup_pe, 1)
            pe.wait_ge(setup_ready, 1)

            def search_tile(entry, which, s, parity, keys):
                if not (isinstance(entry, int) and entry < 2):
                    pe.wait_ge(max_taken, entry - 1)
                mm(max_bank[which][:, :], search_q[:, parity, s * PART:(s + 1) * PART], keys,
                   start=True, stop=True).then_inc(max_ready, 1)

            def shift_row(b, j, parity):
                kb = b * BLOCKS + j
                pe.wait_ge(row_max_ready, kb + 1)
                pe.wait_ge(max_taken, kb * ENTRIES + MAXES)
                for s in range(SUBS):
                    last = mm(max_bank[(parity + MAXES) % 2][0:1, s * PART:(s + 1) * PART],
                              row_max[:, s:s + 1], neg_ident[:, :], start=True, stop=True)
                last.then_inc(max_ready, 1)

            def project_half(b, h):
                for u in range(XSLOTS):
                    j = h * XSLOTS + u
                    kb = b * BLOCKS + j
                    parity = u % 2
                    start = isinstance(kb, int) and kb < 2
                    pe.wait_ge(x_loaded[u], 16 * (b * (BLOCKS // XSLOTS) + h + 1))
                    if not start:
                        pe.wait_ge(low_ready, kb - 1)
                    for k in range(KTILES):
                        last = mm(score_bank[parity][:, :], w_tp[:, k, :], x_in[:, u, k, :],
                                  start=k == 0, stop=k == KTILES - 1)
                    last.then_inc(thetaphi_ready, 1)
                    if not start:
                        pe.wait_ge(values_copied, kb - 1)
                    if u < 2 and not (isinstance(b, int) and b == 0):
                        pe.wait_ge(lat_ready, b * BLOCKS)
                        if not isinstance(b, int) or b > 1:
                            pe.wait_ge(clat_ready, (b - 1) * BLOCKS)
                        if not isinstance(b, int) or b > 2:
                            pe.wait_ge(resid_added, KTILES * BLOCKS * (b - 2))
                    for s in range(SUBS):
                        for k in range(KTILES):
                            last = mm(side_bank[parity][:, s * LATENT:(s + 1) * LATENT],
                                      x_in[:, u, k, s * PART:(s + 1) * PART], w_gs[:, k, :],
                                      start=k == 0, stop=k == KTILES - 1)
                    last.then_inc(values_ready, 1)
                    pe.wait_ge(search_q_loaded[0], 16 * (b * (BLOCKS // 2) + 1))
                    pe.wait_ge(high_ready, kb + 1)
                    for s in range(SUBS):
                        search_tile(b * BLOCKS * ENTRIES + j * SUBS + s, s % 2, s, 0, keys_high[:, block_cols(j)])

            def project(b):
                if isinstance(b, int) and b == 0:
                    for h in range(BLOCKS // XSLOTS):
                        project_half(b, h)
                else:
                    with pe.Fori(0, BLOCKS // XSLOTS) as h:
                        project_half(b, h)
                shift_row(b, 0, 0)

            def score(b, j, t):
                mm(score_bank[t % 2][:, :], keys_high[:, t * PART:(t + 1) * PART], queries_flat[:, q_cols(b, j)],
                   start=True, stop=False)
                mm(score_bank[t % 2][:, :], keys_low[:, t * PART:(t + 1) * PART], queries_shift[:, block_cols(j)],
                   start=False, stop=True).then_inc(scores_ready, 1)

            def turn(b, j):
                kb = b * BLOCKS + j
                pe.wait_ge(sums_copied, kb + 1)
                pe.wait_ge(lat_ready, kb)
                for s in range(SUBS):
                    last = nc.tensor.transpose(side_bank[1][:, s * (LATENT + 1):(s + 1) * (LATENT + 1)],
                                               sums_t[:, s * PART:(s + 1) * PART],
                                               ident[0:LATENT + 1, 0:LATENT + 1])
                last.then_inc(sums_turned, 1)

            def concept_step(step, b1, j):
                n1 = b1 * BLOCKS + j
                if step == "enc":
                    pe.wait_ge(lat_low, n1 + 1)
                    mm(side_bank[0][0:64, :], w_to_high[:, :], lat_split[:, :], start=True, stop=False)
                    mm(side_bank[0][0:64, :], w_to_low[:, :], lat_split[:, :], start=False, stop=False)
                    mm(side_bank[0][0:64, :], two_ident[:, :], queries_flat[:, q_cols(b1, j)],
                       start=False, stop=True).then_inc(enc_ready, 1)
                if step == "max":
                    pe.wait_ge(enc_low, n1 + 1)
                    for i in range(2):
                        for h in range(2):
                            s = 2 * i + h
                            last = mm(side_bank[i][:, h * CONCEPTS:(h + 1) * CONCEPTS],
                                      cqueries[:, s * PART:(s + 1) * PART], ckeys_high[:, :], start=True, stop=True)
                        last.then_inc(cmax_ready, 1)
                if step == "shift":
                    pe.wait_ge(crow_max_ready, 2 * (n1 + 1))
                    for s in range(SUBS):
                        last = mm(side_bank[0][0:1, s * PART:(s + 1) * PART], crow_max[:, s:s + 1],
                                  neg_ident[:, :], start=True, stop=True)
                    last.then_inc(cshift_ready, 1)
                if step == "scores":
                    pe.wait_ge(cshift_taken, n1 + 1)
                    for t in range(CTILES):
                        mm(side_bank[1 - t][:, :], ckeys_high[:, t * PART:(t + 1) * PART], cqueries[:, :],
                           start=True, stop=False)
                        mm(side_bank[1 - t][:, :], ckeys_low[:, t * PART:(t + 1) * PART], cqueries_shift[:, :],
                           start=False, stop=True).then_inc(cscores_ready, 1)
                if step == "sums":
                    pe.wait_ge(cprobs_ready, CTILES * (n1 + 1))
                    for t in range(CTILES):
                        last = mm(side_bank[1][0:LATENT + 1, :], cvalues[:, t, :], cprobs[:, t, :],
                                  start=t == 0, stop=t == CTILES - 1)
                    last.then_inc(csums_ready, 1)
                if step == "turn":
                    pe.wait_ge(csums_copied, n1 + 1)
                    for s in range(SUBS):
                        last = nc.tensor.transpose(side_bank[0][:, s * (LATENT + 1):(s + 1) * (LATENT + 1)],
                                                   csums_t[:, s * PART:(s + 1) * PART],
                                                   ident[0:LATENT + 1, 0:LATENT + 1])
                    last.then_inc(csums_turned, 1)

            def output_step(step, n2):
                for k in (step, step + 1):
                    if k == 0:
                        pe.wait_ge(mix_low, n2 + 1)
                    else:
                        pe.wait_ge(resid_added, KTILES * n2 + k - 1) if k >= 2 else None
                    mm(side_bank[1 - k % 2][:, :], w_ot_high[:, k * PART:(k + 1) * PART], mix_split[:, :],
                       start=True, stop=False)
                    mm(side_bank[1 - k % 2][:, :], w_ot_low[:, k * PART:(k + 1) * PART], mix_split[:, :],
                       start=False, stop=True).then_inc(resid_ready, 1)

            def attend(b, j, parity, side, first=False, last=False):
                kb = b * BLOCKS + j
                if first:
                    pe.wait_ge(low_ready, (b + 1) * BLOCKS)
                    pe.wait_ge(values_copied, (b + 1) * BLOCKS)
                    pe.wait_ge(max_taken, (b * BLOCKS + 1) * ENTRIES)
                    for t in range(2):
                        score(b, 0, t)
                done = 0
                for t in range(KEYTILES):
                    n = kb * KEYTILES + t
                    pe.wait_ge(probs_ready, n + 1)
                    if t == 0 and not (isinstance(b, int) and b == 0 and first):
                        pe.wait_ge(sums_copied, kb - 1)
                    mm(sum_bank[parity][0:LATENT + 1, :], values[:, t, :], probs[:, t % NE, :],
                       start=t == 0, stop=t == KEYTILES - 1).then_inc(probs_used, 1)
                    if t + 2 < KEYTILES:
                        score(b, j, t + 2)
                    elif not last:
                        if t + 2 == KEYTILES:
                            pe.wait_ge(max_taken, (kb + 2) * ENTRIES)
                        score(b, j + 1, t + 2 - KEYTILES)
                    if not last:
                        if t == 0:
                            pe.wait_ge(search_q_loaded[1 - parity], next_loaded(b, j, parity))
                        for i in range(done, SEARCHED[t]):
                            search_tile((kb + 1) * ENTRIES + i, (1 - parity + i) % 2, i % SUBS, 1 - parity,
                                        keys_high[:, (i // SUBS) * BLOCK:(i // SUBS + 1) * BLOCK])
                        done = SEARCHED[t]
                        if t == SHIFT_STEP:
                            shift_row(b, j + 1, 1 - parity)
                    if t == TURN_STEP - 1 and not first:
                        if side >= 2:
                            pe.wait_ge(resid_added, KTILES * (kb - 2 * BLOCKS))
                        turn(b, j - 1)
                    if side >= 1 and t in PE_CONCEPT:
                        if PE_CONCEPT[t] == "enc" and not (isinstance(b, int) and first):
                            pe.wait_ge(clat_ready, kb - BLOCKS)
                            if side >= 2:
                                pe.wait_ge(resid_added, KTILES * (kb - 2 * BLOCKS))
                        if PE_CONCEPT[t] == "max":
                            pe.wait_ge(lat_ready, kb)
                        concept_step(PE_CONCEPT[t], b - 1, j)
                    if side >= 2 and t in PE_OUTPUT:
                        if PE_OUTPUT[t] == 0:
                            pe.wait_ge(clat_ready, kb - BLOCKS + 1)
                            pe.wait_ge(csums_copied, kb - BLOCKS + 1)
                        output_step(PE_OUTPUT[t], kb - 2 * BLOCKS)

            def next_loaded(b, j, parity):
                half = (j + 1) // 2 if isinstance(j, int) else ((j + 1) // 2)
                return 16 * (b * (BLOCKS // 2) + half + 1)

            def finish(b):
                if not isinstance(b, int) or b > 1:
                    pe.wait_ge(resid_added, KTILES * BLOCKS * (b - 1))
                turn(b, BLOCKS - 1)

            def tail(j, concept):
                n1 = (BATCH - 1) * BLOCKS + j
                n2 = (BATCH - 2 if concept else BATCH - 1) * BLOCKS + j
                pe.wait_ge(resid_added, KTILES * n2)
                if concept:
                    pe.wait_ge(lat_ready, BATCH * BLOCKS)
                    pe.wait_ge(clat_ready, n1)
                    for step in ("enc", "max", "shift", "scores", "sums", "turn"):
                        concept_step(step, BATCH - 1, j)
                    pe.wait_ge(clat_ready, n1 + 1)
                for step in (0, 2):
                    output_step(step, n2)

            schedule(pe.Fori, project, attend, finish, tail)


TURN_STEP = 4
PE_CONCEPT = {6: "enc", 9: "max", 12: "shift", 14: "scores", 17: "sums", 19: "turn"}
ACT_CONCEPT = {4: "lat", 7: "enc", 15: "probs", 18: "sums"}
DVE_CONCEPT = {5: "lat", 8: "enc", 10: "max", 13: "shift", 20: "normalize"}
PE_OUTPUT = {22: 0, 25: 2}
ACT_OUTPUT = 11
DVE_OUTPUT = {9: "mix", 14: "low", 23: 0, 26: 2}


def kernel(x, L0_conv_concepts, L0_conv_w_theta, L0_conv_w_phi, L0_conv_w_g, L0_conv_w_o,
           L0_conv_gamma_sa, L0_conv_gamma_moca):
    import numpy as np
    import concourse.bacc as bacc
    from concourse import mybir
    from concourse.bass_utils import run_bass_kernel_spmd

    def by_partition(a):
        return np.ascontiguousarray(a.reshape(-1, PART, a.shape[1]).transpose(1, 0, 2))

    x = np.ascontiguousarray(x)
    theta, phi, g, w_o = (np.asarray(a) for a in (L0_conv_w_theta, L0_conv_w_phi, L0_conv_w_g, L0_conv_w_o))
    concepts = np.asarray(L0_conv_concepts)
    arrays = {
        "x": x.reshape(BATCH, CH, PIXELS),
        "w_thetaphi": by_partition(np.concatenate([theta, phi], axis=0).T),
        "w_g": by_partition(g.T),
        "w_o_t": np.ascontiguousarray(w_o.T),
        "w_o": by_partition(w_o),
        "concepts_t": np.ascontiguousarray(concepts.T),
        "concepts": by_partition(concepts),
        "gamma_sa": np.asarray(L0_conv_gamma_sa).reshape(1),
        "gamma_moca": np.asarray(L0_conv_gamma_moca).reshape(1),
        "consts": np.eye(PART, dtype=np.float32),
    }
    nc = bacc.Bacc("TRN2", target_bir_lowering=False, num_devices=1)
    args = {n: nc.dram_tensor(f"in_{n}", a.shape, mybir.dt.from_np(a.dtype), kind="ExternalInput").ap()
            for n, a in arrays.items()}
    out = nc.dram_tensor("out_0", (BATCH, CH, PIXELS), mybir.dt.float32, kind="ExternalOutput").ap()
    attention_kernel(nc, out=out, **args)
    r = run_bass_kernel_spmd(nc, [{f"in_{n}": a for n, a in arrays.items()}], core_ids=[0])
    return r.results[0]["out_0"].reshape(x.shape)
```

```python
import math

import concourse.bass as bass
from concourse import mybir
from contextlib import ExitStack

BATCH, CH, LATENT, CONCEPTS = 8, 512, 64, 256
PIXELS = 64 * 64
PART = 128
BLOCK = 512
BLOCKS = PIXELS // BLOCK
SUBS = BLOCK // PART
KTILES = CH // PART
KEYTILES = PIXELS // PART
CTILES = CONCEPTS // PART
XSLOTS = 2
NE = 4
NL = 2
XPOOL = 2
LEAD = 3

SEARCHES = BLOCKS * SUBS
SHIFT_STEP = 26
SEARCHED = [min(SEARCHES, -(-(t + 1) * SEARCHES // 25)) for t in range(KEYTILES)]
SETUP_STEPS = 6
FIRST = 1
SEARCH_BANKS = 4


def attention_kernel(nc, x, w_thetaphi, w_g, w_o_t, w_o, concepts_t, concepts, gamma_sa, gamma_moca, consts, out):
    fp32 = mybir.dt.float32
    fp32r = mybir.dt.float32r
    ALU = mybir.AluOpType
    ACT = mybir.ActivationFunctionType
    AX = mybir.AxisListType
    ds = bass.ds

    x_view = x.rearrange("b (k p) n -> b p k n", p=PART)
    out_view = out.rearrange("b (k p) n -> b p k n", p=PART)
    lat_dram = nc.dram_tensor("lat_scratch", (BATCH, PIXELS * LATENT), fp32).ap()
    clat_dram = nc.dram_tensor("clat_scratch", (BATCH, PIXELS * LATENT), fp32).ap()
    lat_store = lat_dram.rearrange("b (j s p c) -> b j p s c", j=BLOCKS, s=SUBS, p=PART)
    clat_store = clat_dram.rearrange("b (j s p c) -> b j p s c", j=BLOCKS, s=SUBS, p=PART)
    lat_load = lat_dram.rearrange("b (l n) -> b l n", l=LATENT)
    clat_load = clat_dram.rearrange("b (l n) -> b l n", l=LATENT)

    ctx = ExitStack()
    with ctx:
        def sb(name, shape, dt=fp32):
            return ctx.enter_context(nc.sbuf_tensor(name, shape, dt))

        def bank(name, shape=(PART, 512)):
            return ctx.enter_context(nc.psum_tensor(name, list(shape), fp32))

        def sem(name):
            return ctx.enter_context(nc.semaphore(name))

        ident = sb("ident", [PART, PART])
        neg_ident = sb("neg_ident", [PART, PART], fp32r)
        fold = sb("fold", [PART, LATENT])
        fold_r = sb("fold_r", [PART, LATENT], fp32r)
        ones = sb("ones", [PART, 1])
        gamma = sb("gamma", [PART, 2])
        w_tp_high = sb("w_tp_high", [PART, KTILES, PART], fp32r)
        w_tp_low = sb("w_tp_low", [PART, KTILES, PART], fp32r)
        w_g_split = sb("w_g_split", [PART, KTILES, PART], fp32r)
        w_ot_high = sb("w_ot_high", [PART, CH], fp32r)
        w_ot_low = sb("w_ot_low", [PART, CH], fp32r)
        w_to_high = sb("w_to_high", [PART, LATENT], fp32r)
        w_to_low = sb("w_to_low", [PART, LATENT], fp32r)
        ckeys_high = sb("ckeys_high", [PART, CONCEPTS], fp32r)
        ckeys_low = sb("ckeys_low", [PART, CONCEPTS], fp32r)
        cvalues = sb("cvalues", [PART, CTILES, LATENT + 1])

        x_in = sb("x_in", [PART, XSLOTS, KTILES, BLOCK])
        x_high = sb("x_high", [PART, XSLOTS, KTILES, BLOCK], fp32r)
        x_low = sb("x_low", [PART, KTILES, BLOCK], fp32r)
        queries = sb("queries", [PART, 2, PIXELS], fp32r)
        queries_shift = sb("queries_shift", [PART, PIXELS], fp32r)
        keys_high = sb("keys_high", [PART, PIXELS], fp32r)
        keys_low = sb("keys_low", [PART, PIXELS], fp32r)
        values = sb("values", [PART, KEYTILES, PART], fp32r)
        search_q = sb("search_q", [PART, 2, BLOCK], fp32r)
        tile_max = sb("tile_max", [PART, SUBS, BLOCKS])
        row_max = sb("row_max", [PART, SUBS], fp32r)
        probs = sb("probs", [PART, NE, BLOCK])
        probs_high = sb("probs_high", [PART, NE, BLOCK], fp32r)
        probs_low = sb("probs_low", [PART, NL, BLOCK], fp32r)
        total = sb("total", [PART, BLOCK])
        g_parts = total
        sums_t = sb("sums_t", [PART, BLOCK])
        inv = sb("inv", [PART, SUBS])
        lat_out = sb("lat_out", [PART, SUBS, LATENT])

        lat_in = sb("lat_in", [PART, BLOCK])
        lat_split = sb("lat_split", [PART, BLOCK], fp32r)
        cqueries = sb("cqueries", [PART, BLOCK], fp32r)
        cqueries_shift = sb("cqueries_shift", [PART, BLOCK], fp32r)
        crow_max = sb("crow_max", [PART, SUBS], fp32r)
        cprobs = sb("cprobs", [PART, CTILES, BLOCK])
        csums_t = sums_t[0:LATENT + 1, :]
        cinv = sb("cinv", [PART, SUBS])
        clat_out = sb("clat_out", [PART, SUBS, LATENT])

        mix_in = sb("mix_in", [PART, 2, BLOCK])
        mix_split = sb("mix_split", [PART, BLOCK], fp32r)
        resid = sb("resid", [PART, KTILES, BLOCK])
        raw_tp = resid[:, 0, :].rearrange("p (k c) -> p k c", k=KTILES)
        raw_g = resid[:, 1, 0:KTILES * LATENT].rearrange("p (k c) -> p k c", k=KTILES)
        raw_o = resid[:, 1, KTILES * LATENT:].rearrange("p (k c) -> p k c", k=KTILES)
        raw_ot = resid[:, 2, :]
        raw_ct = resid[:, 3, 0:CONCEPTS]

        score_bank = [bank(f"score_bank{i}") for i in range(2)]
        max_bank = [bank(f"max_bank{i}") for i in range(2)]
        sum_bank = bank("sum_bank")
        total_bank = bank("total_bank")
        side_bank = [bank(f"side_bank{i}") for i in range(2)]
        first_search_bank = max_bank + [sum_bank, total_bank]

        consts_in, weights_in = sem("consts_in"), sem("weights_in")
        x_loaded = [sem(f"x_loaded{i}") for i in range(XSLOTS)]
        search_q_loaded = [sem(f"search_q_loaded{i}") for i in range(2)]
        lat_stored, clat_stored, out_stored = sem("lat_stored"), sem("clat_stored"), sem("out_stored")
        lat_loaded, mix_loaded, resid_loaded = sem("lat_loaded"), sem("mix_loaded"), sem("resid_loaded")
        setup_dve, setup_pe, setup_ready = sem("setup_dve"), sem("setup_pe"), sem("setup_ready")
        x_high_ready, x_low_pool, x_low_dve = sem("x_high_ready"), sem("x_low_pool"), sem("x_low_dve")
        thetaphi_ready, g_ready, g_copied = sem("thetaphi_ready"), sem("g_ready"), sem("g_copied")
        g_turned, values_high_ready, values_ready = sem("g_turned"), sem("values_high_ready"), sem("values_ready")
        high_ready, low_ready = sem("high_ready"), sem("low_ready")
        max_ready, max_taken = sem("max_ready"), sem("max_taken")
        row_max_ready, shift_ready, shift_taken = sem("row_max_ready"), sem("shift_ready"), sem("shift_taken")
        scores_ready, probs_ready, probs_high_ready = sem("scores_ready"), sem("probs_ready"), sem("probs_high_ready")
        probs_low_ready, probs_added, probs_used = sem("probs_low_ready"), sem("probs_added"), sem("probs_used")
        sums_copied, sums_turned = sem("sums_copied"), sem("sums_turned")
        inv_ready, lat_ready = sem("inv_ready"), sem("lat_ready")
        lat_high, lat_low = sem("lat_high"), sem("lat_low")
        enc_ready, enc_high, enc_low = sem("enc_ready"), sem("enc_high"), sem("enc_low")
        cmax_ready, crow_max_ready = sem("cmax_ready"), sem("crow_max_ready")
        cshift_ready, cshift_taken = sem("cshift_ready"), sem("cshift_taken")
        cscores_ready, cprobs_ready = sem("cscores_ready"), sem("cprobs_ready")
        csums_ready, csums_copied, csums_turned = sem("csums_ready"), sem("csums_copied"), sem("csums_turned")
        cinv_ready, clat_ready = sem("cinv_ready"), sem("clat_ready")
        mix_added, mix_high, mix_low = sem("mix_added"), sem("mix_high"), sem("mix_low")
        resid_ready, resid_added = sem("resid_ready"), sem("resid_added")

        raw = lambda ap: ap.bitcast(fp32)

        def block_cols(j):
            return ds(j * BLOCK, BLOCK) if not isinstance(j, int) else slice(j * BLOCK, (j + 1) * BLOCK)

        def q_cols(b, j):
            at = (b % 2) * PIXELS + j * BLOCK
            return ds(at, BLOCK) if not isinstance(at, int) else slice(at, at + BLOCK)

        queries_flat = queries[:, :, :].rearrange("p a n -> p (a n)")

        g_by_key = side_bank[1][:, 0:SUBS * LATENT].rearrange("p (s c) -> p s c", s=SUBS)

        def tiles_of(j):
            return slice(j * SUBS, (j + 1) * SUBS) if isinstance(j, int) else ds(j * SUBS, SUBS)

        def x_count(b, j):
            half = j // XSLOTS if isinstance(j, int) else j // XSLOTS
            return 16 * (b * (BLOCKS // XSLOTS) + half + 1)

        def schedule(loop, project, attend, finish, tail):
            def batch(b, side):
                project(b, 0, 0)
                with loop(0, (BLOCKS - 4) // 2) as pair:
                    project(b, 2 * pair + 1, 1)
                    project(b, 2 * pair + 2, 0)
                for j in range(BLOCKS - 3, BLOCKS):
                    project(b, j, j % 2)
                attend(b, 0, 0, side, first=True)
                with loop(0, (BLOCKS - 2) // 2) as pair:
                    attend(b, 2 * pair + 1, 1, side)
                    attend(b, 2 * pair + 2, 0, side)
                attend(b, BLOCKS - 1, 1, side, last=True)
                finish(b)

            batch(0, 0)
            batch(1, 1)
            with loop(2, BATCH - 1) as b:
                batch(b, 2)
            batch(BATCH - 1, 2)
            with loop(0, BLOCKS) as j:
                tail(j, True)
            with loop(0, BLOCKS) as j:
                tail(j, False)

        def splits_ahead(b, j):
            return not (is_last(b) and isinstance(j, int) and j >= BLOCKS - XSLOTS)

        def has_next(b, j):
            return not (is_last(b) and isinstance(j, int) and j == BLOCKS - 1)

        def is_last(b):
            return isinstance(b, int) and b == BATCH - 1

        block = ctx.enter_context(nc.Block())

        @block.sync
        def _(sp):
            def load_x(b, j, slot):
                src = x_view[ds(b, 1), :, :, block_cols(j)].rearrange("a p k n -> (a p) k n")
                sp.dma_start(x_in[:, slot, :, :], src).then_inc(x_loaded[slot], 16)

            def load_search_q(b, j, parity):
                sp.dma_start(raw(search_q[:, parity, :]), raw(queries_flat[:, q_cols(b, j)]))\
                  .then_inc(search_q_loaded[parity], 16)

            sp.dma_start(ident[:, :], consts).then_inc(consts_in, 16)

            def counted(value):
                return value if isinstance(value, int) else sp.snap(value)

            def project(b):
                for j in range(BLOCKS):
                    if splits_ahead(b, j):
                        split = counted(b * BLOCKS + j + 1)
                        sp.wait_ge(x_low_pool, split)
                        sp.wait_ge(x_low_dve, split)
                        load_x(b + (j + XSLOTS) // BLOCKS, (j + XSLOTS) % BLOCKS, j % XSLOTS)
                    if j < 2:
                        sp.wait_ge(low_ready, b * BLOCKS + j + 1 + FIRST)
                        load_search_q(b, j, j)

            def load_side(b, j, side):
                n1 = counted((b - 1) * BLOCKS + j + FIRST)
                if side >= 1:
                    sp.wait_ge(lat_stored, 16 * BLOCKS * b + FIRST)
                    sp.wait_ge(lat_low, n1)
                    src = lat_load[ds(b - 1, 1), :, block_cols(j)].rearrange("a l n -> (a l) n")
                    sp.dma_start(lat_in[0:64, :], src).then_inc(lat_loaded, 16)
                    sp.dma_start(lat_in[64:128, :], src).then_inc(lat_loaded, 16)
                if side >= 2:
                    load_output(b - 2, j)

            def load_output(b2, j):
                mixed = counted(b2 * BLOCKS + j + FIRST)
                left = counted(16 * (b2 * BLOCKS + j) + FIRST)
                sp.wait_ge(mix_low, mixed)
                sp.wait_ge(clat_stored, 16 * BLOCKS * (b2 + 1) + FIRST)
                for half in (0, 64):
                    for i, view in enumerate((lat_load, clat_load)):
                        src = view[ds(b2, 1), :, block_cols(j)].rearrange("a l n -> (a l) n")
                        sp.dma_start(mix_in[half:half + 64, i, :], src).then_inc(mix_loaded, 16)
                sp.wait_ge(out_stored, left)
                src = x_view[ds(b2, 1), :, :, block_cols(j)].rearrange("a p k n -> (a p) k n")
                sp.dma_start(resid[:, :, :], src).then_inc(resid_loaded, 16)

            def store_lat(b, j):
                sp.wait_ge(lat_ready, b * BLOCKS + j + 1 + FIRST)
                dst = lat_store[ds(b, 1), ds(j, 1), :, :, :].rearrange("a j p s c -> (a j p) s c")
                sp.dma_start(dst, lat_out[:, :, :]).then_inc(lat_stored, 16)

            def store_clat(b1, j):
                sp.wait_ge(clat_ready, b1 * BLOCKS + j + 1 + FIRST)
                dst = clat_store[ds(b1, 1), ds(j, 1), :, :, :].rearrange("a j p s c -> (a j p) s c")
                sp.dma_start(dst, clat_out[:, :, :]).then_inc(clat_stored, 16)

            def store_out(b2, j):
                sp.wait_ge(resid_added, KTILES * (b2 * BLOCKS + j + 1) + FIRST)
                dst = out_view[ds(b2, 1), :, :, block_cols(j)].rearrange("a p k n -> (a p) k n")
                sp.dma_start(dst, resid[:, :, :]).then_inc(out_stored, 16)

            def load_next(b, j):
                sp.wait_ge(max_ready, (b * BLOCKS + j + 1) * SEARCHES)
                load_search_q(b, j + 2, j % 2)

            def attend(b, j, side):
                load_side(b, j, side)
                if j < BLOCKS - 2:
                    load_next(b, j)
                if j > 0:
                    store_lat(b, j - 1)
                if side >= 1:
                    store_clat(b - 1, j)
                if side >= 2:
                    store_out(b - 2, j)

            def batch(b, side):
                project(b)
                for j in range(BLOCKS):
                    attend(b, j, side)
                store_lat(b, BLOCKS - 1)

            for u in range(XSLOTS):
                load_x(0, u, u)
            for dst, src in ((raw_tp[:, :, :], w_thetaphi), (raw_g[:, :, :], w_g), (raw_o[:, :, :], w_o),
                             (cvalues[:, :, 0:LATENT], concepts),
                             (raw_ot[0:64, :], w_o_t), (raw_ot[64:128, :], w_o_t),
                             (raw_ct[0:64, :], concepts_t), (raw_ct[64:128, :], concepts_t),
                             (gamma[:, 0:1], gamma_sa.partition_broadcast(PART)),
                             (gamma[:, 1:2], gamma_moca.partition_broadcast(PART))):
                sp.dma_start(dst, src).then_inc(weights_in, 16)
            batch(0, 0)
            batch(1, 1)
            with sp.Fori(2, BATCH - 1) as b:
                batch(b, 2)
            batch(BATCH - 1, 2)
            with sp.Fori(0, BLOCKS) as j:
                load_side(BATCH, j, 2)
                store_clat(BATCH - 1, j)
                store_out(BATCH - 2, j)
            with sp.Fori(0, BLOCKS) as j:
                load_output(BATCH - 1, j)
                store_out(BATCH - 1, j)
            sp.wait_ge(lat_stored, 16 * BATCH * BLOCKS + FIRST)
            sp.wait_ge(clat_stored, 16 * BATCH * BLOCKS + FIRST)
            sp.wait_ge(out_stored, 16 * BATCH * BLOCKS + FIRST)

        @block.gpsimd
        def _(pool):
            def split_x(kb, slot):
                pool.wait_ge(x_high_ready, kb + 1)
                nc.gpsimd.tensor_tensor(x_low[:, 0:XPOOL, :], x_in[:, slot, 0:XPOOL, :],
                                        raw(x_high[:, slot, 0:XPOOL, :]), ALU.subtract).then_inc(x_low_pool, 1)

            def project(b, j, parity):
                if has_next(b, j):
                    pool.wait_ge(g_ready, b * BLOCKS + j + 1)
                    split_x(b * BLOCKS + j + 1, 1 - parity)

            def split_probs(b, j, t):
                n = (b * BLOCKS + j) * KEYTILES + t
                pool.wait_ge(probs_high_ready, n + 1)
                if not (isinstance(n, int) and n < NL):
                    pool.wait_ge(probs_used, n - NL + 1)
                nc.gpsimd.tensor_tensor(probs_low[:, t % NL, :], probs[:, t % NE, :],
                                        raw(probs_high[:, t % NE, :]), ALU.subtract).then_inc(probs_low_ready, 1)

            def lat_step(n1):
                pool.wait_ge(lat_high, n1 + 1)
                nc.gpsimd.tensor_tensor(lat_split[64:128, :], lat_in[64:128, :], raw(lat_split[64:128, :]),
                                        ALU.subtract).then_inc(lat_low, 1)

            def mix_step(n2):
                pool.wait_ge(mix_loaded, 64 * (n2 + 1))
                nc.gpsimd.tensor_tensor(mix_in[:, 0, :], mix_in[:, 0, :], mix_in[:, 1, :], ALU.add)\
                    .then_inc(mix_added, 1)

            def mix_low_step(n2):
                pool.wait_ge(mix_high, n2 + 1)
                nc.gpsimd.tensor_tensor(mix_split[64:128, :], mix_in[64:128, 0, :], raw(mix_split[64:128, :]),
                                        ALU.subtract).then_inc(mix_low, 1)

            def attend(b, j, parity, side, first=False, last=False):
                n = b * BLOCKS + j
                for t in range(KEYTILES):
                    split_probs(b, j, t)
                    if side >= 1 and t == POOL_CONCEPT:
                        pool.wait_ge(probs_low_ready, n * KEYTILES + t + 1)
                        lat_step(n - BLOCKS)
                        pool.wait_ge(lat_low, n - BLOCKS + 1 + FIRST)
                    if side >= 2 and t == POOL_OUTPUT["mix"]:
                        mix_step(n - 2 * BLOCKS)
                    if side >= 2 and t == POOL_OUTPUT["low"]:
                        pool.wait_ge(probs_low_ready, n * KEYTILES + t + 1)
                        mix_low_step(n - 2 * BLOCKS)
                        pool.wait_ge(mix_low, n - 2 * BLOCKS + 1 + FIRST)

            def tail(j, concept):
                n2 = (BATCH - 2 if concept else BATCH - 1) * BLOCKS + j
                pool.wait_ge(mix_low, n2 + FIRST)
                if concept:
                    lat_step((BATCH - 1) * BLOCKS + j)
                    pool.wait_ge(lat_low, (BATCH - 1) * BLOCKS + j + 1 + FIRST)
                mix_step(n2)
                mix_low_step(n2)

            split_x(0, 0)
            schedule(pool.Fori, project, attend, lambda b: None, tail)

        @block.scalar
        def _(act):
            def split_x(kb, slot):
                act.wait_ge(x_loaded[slot], 16 * (kb // XSLOTS + 1))
                nc.scalar.activation(x_high[:, slot, :, :], x_in[:, slot, :, :], ACT.Copy).then_inc(x_high_ready, 1)

            def copy_values(b, j):
                kb = b * BLOCKS + j
                act.wait_ge(g_turned, kb + 1)
                nc.scalar.activation(values[:, tiles_of(j), 0:LATENT], g_by_key, ACT.Copy)\
                    .then_inc(values_high_ready, 1)

            def project(b, j, parity):
                kb = b * BLOCKS + j
                if not (isinstance(j, int) and j == 0):
                    copy_values(b, j - 1)
                tp = score_bank[parity]
                act.wait_ge(thetaphi_ready, kb + 1)
                nc.scalar.activation(keys_high[0:64, block_cols(j)], tp[64:128, :], ACT.Copy)
                nc.scalar.activation(keys_high[64:128, block_cols(j)], tp[64:128, :], ACT.Copy)
                nc.scalar.activation(queries_flat[0:64, q_cols(b, j)], tp[0:64, :], ACT.Copy)
                nc.scalar.activation(queries_shift[0:64, block_cols(j)], tp[0:64, :], ACT.Copy)\
                    .then_inc(high_ready, 1)
                act.wait_ge(g_ready, kb + 1)
                if splits_ahead(b, j):
                    act.wait_ge(x_loaded[parity], x_count(b, j + XSLOTS))
                    nc.scalar.activation(x_high[:, parity, :, :], x_in[:, parity, :, :], ACT.Copy)\
                        .then_inc(x_high_ready, 1)
                act.wait_ge(g_turned, kb)
                nc.scalar.activation(g_parts[:, :], side_bank[0][:, :], ACT.Copy).then_inc(g_copied, 1)

            def copy_sums(b, j):
                kb = b * BLOCKS + j
                act.wait_ge(probs_used, (kb + 1) * KEYTILES)
                act.wait_ge(sums_turned, kb + FIRST)
                nc.scalar.activation(sums_t[:, :], sum_bank[:, :], ACT.Copy).then_inc(sums_copied, 1)

            def copy_shift(b, j):
                act.wait_ge(shift_ready, b * BLOCKS + j + 1)
                nc.scalar.activation(queries_shift[64:65, block_cols(j)], max_bank[0][0:1, :], ACT.Copy)\
                    .then_inc(shift_taken, 1)

            def exp_scores(b, j, t):
                n = (b * BLOCKS + j) * KEYTILES + t
                started = not (isinstance(n, int) and n < NE)
                act.wait_ge(scores_ready, n + 1)
                if started:
                    act.wait_ge(probs_low_ready, n - NE + 1)
                    act.wait_ge(probs_added, n - NE + 1)
                nc.scalar.activation(probs[:, t % NE, :], score_bank[t % 2][:, :], ACT.Exp).then_inc(probs_ready, 1)
                if started:
                    act.wait_ge(probs_used, n - NE + 1)
                nc.scalar.activation(probs_high[:, t % NE, :], score_bank[t % 2][:, :], ACT.Exp)\
                    .then_inc(probs_high_ready, 1)

            def concept_step(step, n1):
                if step == "lat":
                    act.wait_ge(lat_loaded, 32 * (n1 + 1))
                    nc.scalar.activation(lat_split[:, :], lat_in[:, :], ACT.Copy).then_inc(lat_high, 1)
                if step == "enc":
                    act.wait_ge(enc_ready, n1 + 1)
                    nc.scalar.activation(cqueries[0:64, :], side_bank[0][0:64, :], ACT.Copy)
                    nc.scalar.activation(cqueries_shift[0:64, :], side_bank[0][0:64, :], ACT.Copy)\
                        .then_inc(enc_high, 1)
                if step == "shift":
                    act.wait_ge(cshift_ready, n1 + 1)
                    nc.scalar.activation(cqueries_shift[64:65, :], side_bank[0][0:1, :], ACT.Copy)\
                        .then_inc(cshift_taken, 1)
                if step == "probs":
                    for t in range(CTILES):
                        act.wait_ge(cscores_ready, CTILES * n1 + t + 1)
                        nc.scalar.activation(cprobs[:, t, :], side_bank[1 - t][:, :], ACT.Exp)\
                            .then_inc(cprobs_ready, 1)
                if step == "sums":
                    act.wait_ge(csums_ready, n1 + 1)
                    nc.scalar.activation(csums_t[:, :], side_bank[1][0:LATENT + 1, :], ACT.Copy)\
                        .then_inc(csums_copied, 1)

            def output_step(n2):
                act.wait_ge(mix_added, n2 + 1)
                nc.scalar.activation(mix_split[:, :], mix_in[:, 0, :], ACT.Copy).then_inc(mix_high, 1)

            def attend(b, j, parity, side, first=False, last=False):
                n = b * BLOCKS + j
                if first:
                    copy_values(b, BLOCKS - 1)
                    copy_shift(b, 0)
                for t in range(KEYTILES):
                    if t == LEAD - 1 and not first:
                        copy_sums(b, j - 1)
                    exp_scores(b, j, t)
                    if t == SHIFT_STEP + LEAD - 1 and not last:
                        copy_shift(b, j + 1)
                    if side >= 1 and t in ACT_CONCEPT:
                        concept_step(ACT_CONCEPT[t], n - BLOCKS)
                    if side >= 2 and t == ACT_OUTPUT:
                        output_step(n - 2 * BLOCKS)

            def tail(j, concept):
                if concept:
                    for step in ("lat", "enc", "shift", "probs", "sums"):
                        concept_step(step, (BATCH - 1) * BLOCKS + j)
                output_step((BATCH - 2 if concept else BATCH - 1) * BLOCKS + j)

            for u in range(XSLOTS):
                split_x(u, u)
            schedule(act.Fori, project, attend, lambda b: copy_sums(b, BLOCKS - 1), tail)

        @block.vector
        def _(dve):
            steps = [0]

            def then(ins):
                steps[0] += 1
                ins.then_inc(setup_dve, 1)
                dve.wait_ge(setup_dve, steps[0])

            def split_x(kb, slot):
                dve.wait_ge(x_high_ready, kb + 1)
                nc.vector.tensor_tensor(x_low[:, XPOOL:KTILES, :], x_in[:, slot, XPOOL:KTILES, :],
                                        raw(x_high[:, slot, XPOOL:KTILES, :]), ALU.subtract).then_inc(x_low_dve, 1)

            gain = float(1.0 / math.sqrt(CH))
            out_gain = float(1.0 / math.sqrt(LATENT))
            released = (lat_ready, lat_stored, clat_ready, clat_stored, out_stored, lat_low, mix_low,
                        resid_added, sums_copied, sums_turned, low_ready, values_ready)
            for i, buffer in enumerate(released):
                nc.vector.memset(tile_max[:, i // BLOCKS, i % BLOCKS:i % BLOCKS + 1], 0.0).then_inc(buffer, FIRST)
            nc.vector.memset(tile_max[:, SUBS - 1, :], 0.0).then_inc(max_taken, SEARCH_BANKS)
            nc.vector.memset(raw(keys_low[64:128, :]), 0.0)
            nc.vector.memset(raw(queries_shift[64:128, :]), 0.0)
            nc.vector.memset(raw(ckeys_low[64:128, :]), 0.0)
            nc.vector.memset(raw(cqueries_shift[64:128, :]), 0.0)
            nc.vector.memset(ones[:, :], 1.0)
            then(nc.vector.memset(cvalues[:, :, LATENT:LATENT + 1], 1.0))
            nc.vector.memset(raw(keys_low[64:65, :]), 1.0)
            then(nc.vector.memset(raw(ckeys_low[64:65, :]), 1.0))
            split_x(0, 0)
            dve.wait_ge(consts_in, 16)
            nc.vector.tensor_scalar(neg_ident[:, :], ident[:, :], -1.0, None, ALU.mult)
            for half in (0, 64):
                for folded in (fold, fold_r):
                    nc.vector.tensor_copy(folded[half:half + 64, :], ident[half:half + 64, half:half + 64])
            dve.wait_ge(weights_in, 16 * 10)
            nc.vector.tensor_scalar(raw_tp[:, :, :], raw_tp[:, :, :], gain, None, ALU.mult)
            nc.vector.tensor_scalar(raw_g[:, :, :], raw_g[:, :, :], gain, None, ALU.mult)
            nc.vector.tensor_scalar(raw_o[:, :, :], raw_o[:, :, :], out_gain, None, ALU.mult)
            nc.vector.tensor_scalar(raw_ot[:, :], raw_ot[:, :], out_gain, None, ALU.mult)
            nc.vector.tensor_scalar(cvalues[:, :, 0:LATENT], cvalues[:, :, 0:LATENT], gamma[:, 1:2], None, ALU.mult)
            then(nc.vector.tensor_copy(ckeys_high[:, :], raw_ct[:, :]))
            nc.vector.tensor_scalar(raw_g[:, :, :], raw_g[:, :, :], gamma[:, 0:1], None, ALU.mult)
            nc.vector.tensor_copy(w_tp_high[:, :, :], raw_tp[:, :, :])
            then(nc.vector.tensor_copy(w_ot_high[:, :], raw_ot[:, :]))
            nc.vector.tensor_tensor(w_tp_low[:, :, :], raw_tp[:, :, :], raw(w_tp_high[:, :, :]), ALU.subtract)
            nc.vector.tensor_copy(w_g_split[:, :, 0:LATENT], raw_g[:, :, :])
            nc.vector.tensor_tensor(w_ot_low[:, :], raw_ot[:, :], raw(w_ot_high[:, :]), ALU.subtract)
            then(nc.vector.tensor_tensor(ckeys_low[0:64, :], raw_ct[0:64, :], raw(ckeys_high[0:64, :]), ALU.subtract))
            then(nc.vector.tensor_tensor(w_g_split[:, :, LATENT:PART], raw_g[:, :, :],
                                         raw(w_g_split[:, :, 0:LATENT]), ALU.subtract))
            assert steps[0] == SETUP_STEPS
            dve.wait_ge(setup_pe, 1)
            product = side_bank[0][0:64, 0:LATENT]
            nc.vector.tensor_copy(w_to_high[0:64, :], product)
            then(nc.vector.tensor_copy(w_to_high[64:128, :], product))
            nc.vector.tensor_tensor(w_to_low[0:64, :], product, raw(w_to_high[0:64, :]), ALU.subtract)
            nc.vector.tensor_tensor(w_to_low[64:128, :], product, raw(w_to_high[0:64, :]), ALU.subtract)\
                .then_inc(setup_ready, 1)

            def take_max(entry, out, searched):
                dve.wait_ge(max_ready, entry + 1)
                nc.vector.reduce_max(out, searched[:, :], AX.X).then_inc(max_taken, 1)

            def finish_max(kb):
                dve.wait_ge(max_taken, (kb + 1) * SEARCHES + SEARCH_BANKS)
                nc.vector.tensor_reduce(row_max[:, :], tile_max[:, :, :], AX.X, ALU.max).then_inc(row_max_ready, 1)

            def first_search(b, j):
                for s in range(SUBS):
                    at = slice(j, j + 1) if isinstance(j, int) else ds(j, 1)
                    take_max(b * BLOCKS * SEARCHES + j * SUBS + s, tile_max[:, s, at], first_search_bank[s])

            def low_values(b, j):
                kb = b * BLOCKS + j
                dve.wait_ge(values_high_ready, kb + 1)
                nc.vector.tensor_tensor(values[:, tiles_of(j), LATENT:PART], g_by_key,
                                        raw(values[:, tiles_of(j), 0:LATENT]), ALU.subtract)\
                    .then_inc(values_ready, 1)

            def project(b, j, parity):
                kb = b * BLOCKS + j
                tp = score_bank[parity]
                if not (isinstance(j, int) and j == 0):
                    first_search(b, j - 1)
                    low_values(b, j - 1)
                dve.wait_ge(high_ready, kb + 1)
                nc.vector.tensor_tensor(queries_flat[64:128, q_cols(b, j)], tp[0:64, :],
                                        raw(queries_flat[0:64, q_cols(b, j)]), ALU.subtract)
                nc.vector.tensor_tensor(keys_low[0:64, block_cols(j)], tp[64:128, :],
                                        raw(keys_high[64:128, block_cols(j)]), ALU.subtract).then_inc(low_ready, 1)
                if has_next(b, j):
                    dve.wait_ge(g_ready, kb + 1)
                    split_x(kb + 1, 1 - parity)

            def add_probs(b, j, t):
                kb = b * BLOCKS + j
                n = kb * KEYTILES + t
                if t == 0:
                    return
                dve.wait_ge(probs_ready, n + 1)
                if t == 1:
                    if not (isinstance(kb, int) and kb == 0):
                        dve.wait_ge(probs_added, kb * KEYTILES)
                    nc.vector.tensor_tensor(total_bank[:, :], probs[:, 0, :], probs[:, 1, :], ALU.add)\
                        .then_inc(probs_added, 2)
                    return
                dve.wait_ge(probs_added, n)
                if t == KEYTILES - 1:
                    dve.wait_ge(sums_turned, kb + FIRST)
                nc.vector.tensor_tensor(total[:, :] if t == KEYTILES - 1 else total_bank[:, :], total_bank[:, :],
                                        probs[:, t % NE, :], ALU.add).then_inc(probs_added, 1)

            def normalize(b, j):
                kb = b * BLOCKS + j
                turned = side_bank[1][:, 0:SUBS * (LATENT + 1)].rearrange("p (s c) -> p s c", s=SUBS)
                dve.wait_ge(sums_turned, kb + 1 + FIRST)
                nc.vector.reciprocal(inv[:, :], turned[:, :, LATENT]).then_inc(inv_ready, 1)
                dve.wait_ge(inv_ready, kb + 1)
                dve.wait_ge(lat_stored, 16 * kb + FIRST)
                nc.vector.tensor_tensor(lat_out[:, :, :], turned[:, :, 0:LATENT],
                                        inv[:, :].unsqueeze(2).to_broadcast([PART, SUBS, LATENT]), ALU.mult)\
                    .then_inc(lat_ready, 1)

            def concept_step(step, n1):
                if step == "enc":
                    dve.wait_ge(enc_high, n1 + 1)
                    nc.vector.tensor_tensor(cqueries[64:128, :], side_bank[0][0:64, :], raw(cqueries[0:64, :]),
                                            ALU.subtract).then_inc(enc_low, 1)
                if step == "max":
                    for i in range(2):
                        dve.wait_ge(cmax_ready, 2 * n1 + i + 1)
                        nc.vector.tensor_reduce(crow_max[:, 2 * i:2 * i + 2],
                                                side_bank[i][:, :].rearrange("p (s m) -> p s m", s=2),
                                                AX.X, ALU.max).then_inc(crow_max_ready, 1)
                if step == "normalize":
                    turned = side_bank[0][:, 0:SUBS * (LATENT + 1)].rearrange("p (s c) -> p s c", s=SUBS)
                    dve.wait_ge(csums_turned, n1 + 1)
                    nc.vector.reciprocal(cinv[:, :], turned[:, :, LATENT]).then_inc(cinv_ready, 1)
                    dve.wait_ge(cinv_ready, n1 + 1)
                    dve.wait_ge(clat_stored, 16 * n1 + FIRST)
                    nc.vector.tensor_tensor(clat_out[:, :, :], turned[:, :, 0:LATENT],
                                            cinv[:, :].unsqueeze(2).to_broadcast([PART, SUBS, LATENT]), ALU.mult)\
                        .then_inc(clat_ready, 1)

            def output_step(step, n2):
                for k in (step, step + 1):
                    if k == 0:
                        dve.wait_ge(resid_loaded, 16 * (n2 + 1))
                    dve.wait_ge(resid_ready, KTILES * n2 + k + 1)
                    nc.vector.tensor_tensor(resid[:, k, :], resid[:, k, :], side_bank[1 - k % 2][:, :], ALU.add)\
                        .then_inc(resid_added, 1)

            def attend(b, j, parity, side, first=False, last=False):
                n = b * BLOCKS + j
                if first:
                    first_search(b, BLOCKS - 1)
                    finish_max(n)
                    low_values(b, BLOCKS - 1)
                done = 0
                for t in range(KEYTILES):
                    add_probs(b, j, t)
                    if not last:
                        for i in range(done, SEARCHED[t]):
                            take_max((n + 1) * SEARCHES + i, tile_max[:, i % SUBS, i // SUBS:i // SUBS + 1],
                                     max_bank[i % 2])
                        if done < SEARCHES == SEARCHED[t]:
                            finish_max(n + 1)
                        done = SEARCHED[t]
                    if t == TURN_STEP and not first:
                        normalize(b, j - 1)
                    if side >= 1 and t in DVE_CONCEPT:
                        concept_step(DVE_CONCEPT[t], n - BLOCKS)
                    if side >= 2 and t in DVE_OUTPUT:
                        output_step(DVE_OUTPUT[t], n - 2 * BLOCKS)

            def tail(j, concept):
                if concept:
                    for step in ("enc", "max", "normalize"):
                        concept_step(step, (BATCH - 1) * BLOCKS + j)
                for step in (0, 2):
                    output_step(step, (BATCH - 2 if concept else BATCH - 1) * BLOCKS + j)

            schedule(dve.Fori, project, attend, lambda b: normalize(b, BLOCKS - 1), tail)

        @block.tensor
        def _(pe):
            mm = nc.tensor.matmul
            pe.wait_ge(setup_dve, SETUP_STEPS)
            for k in range(KTILES):
                last = mm(side_bank[0][0:64, 0:LATENT], raw_o[:, k, :], raw_tp[:, k, 0:LATENT],
                          start=k == 0, stop=k == KTILES - 1)
            last.then_inc(setup_pe, 1)
            pe.wait_ge(setup_ready, 1)

            def first_search(b, j, s):
                entry = b * BLOCKS * SEARCHES + j * SUBS + s
                pe.wait_ge(high_ready, b * BLOCKS + j + 1)
                pe.wait_ge(max_taken, entry + 1)
                mm(first_search_bank[s][:, :], search_q[:, 0, s * PART:(s + 1) * PART], keys_high[:, block_cols(j)],
                   start=True, stop=True).then_inc(max_ready, 1)

            def search(kb, parity, i):
                entry = kb * SEARCHES + i
                pe.wait_ge(max_taken, entry - 1 + SEARCH_BANKS)
                mm(max_bank[i % 2][:, :], search_q[:, parity, (i % SUBS) * PART:(i % SUBS + 1) * PART],
                   keys_high[:, (i // SUBS) * BLOCK:(i // SUBS + 1) * BLOCK], start=True, stop=True)\
                    .then_inc(max_ready, 1)

            def shift_row(kb):
                pe.wait_ge(row_max_ready, kb + 1)
                for s in range(SUBS):
                    last = mm(max_bank[0][0:1, s * PART:(s + 1) * PART], row_max[:, s:s + 1], neg_ident[:, :],
                              start=True, stop=True)
                last.then_inc(shift_ready, 1)

            def turn_g(b, j):
                kb = b * BLOCKS + j
                pe.wait_ge(g_copied, kb + 1)
                pe.wait_ge(values_ready, kb + FIRST)
                for s in range(SUBS):
                    last = mm(side_bank[1][:, s * LATENT:(s + 1) * LATENT], g_parts[:, s * PART:(s + 1) * PART],
                              fold[:, :], start=True, stop=True)
                last.then_inc(g_turned, 1)

            def project(b, j, parity):
                kb = b * BLOCKS + j
                first = isinstance(j, int) and j == 0
                tp, g = score_bank[parity], side_bank[0]
                high = x_high[:, parity, :, :]

                def product(out, weights, part, start=False, stop=False):
                    for k in range(KTILES):
                        last = mm(out[:, :], weights[:, k, :], part[:, k, :],
                                  start=start and k == 0, stop=stop and k == KTILES - 1)
                    return last

                pe.wait_ge(x_high_ready, kb + 1)
                pe.wait_ge(low_ready, kb - 1 + FIRST)
                product(tp, w_tp_high, high, start=True)
                product(tp, w_tp_low, high)
                if first:
                    pe.wait_ge(lat_ready, b * BLOCKS + FIRST)
                    if not isinstance(b, int) or b > 1:
                        pe.wait_ge(clat_ready, (b - 1) * BLOCKS + FIRST)
                else:
                    pe.wait_ge(search_q_loaded[0], 16 * (b * (BLOCKS // 2) + 1))
                    first_search(b, j - 1, 0)
                pe.wait_ge(g_copied, kb) if not (isinstance(kb, int) and kb == 0) else None
                product(g, w_g_split, high, start=True)
                if not first:
                    first_search(b, j - 1, 1)
                    turn_g(b, j - 1)
                pe.wait_ge(x_low_pool, kb + 1)
                pe.wait_ge(x_low_dve, kb + 1)
                product(tp, w_tp_high, x_low, stop=True).then_inc(thetaphi_ready, 1)
                if not first:
                    first_search(b, j - 1, 2)
                product(g, w_g_split, x_low, stop=True).then_inc(g_ready, 1)
                if not first:
                    first_search(b, j - 1, 3)

            def score(b, j, t):
                mm(score_bank[t % 2][:, :], keys_high[:, t * PART:(t + 1) * PART], queries_flat[:, q_cols(b, j)],
                   start=True, stop=False)
                mm(score_bank[t % 2][:, :], keys_low[:, t * PART:(t + 1) * PART], queries_shift[:, block_cols(j)],
                   start=False, stop=True).then_inc(scores_ready, 1)

            def turn(b, j):
                kb = b * BLOCKS + j
                pe.wait_ge(sums_copied, kb + 1 + FIRST)
                pe.wait_ge(probs_added, (kb + 1) * KEYTILES)
                pe.wait_ge(lat_ready, kb + FIRST)
                for s in range(SUBS):
                    at = s * (LATENT + 1)
                    mm(side_bank[1][:, at:at + LATENT], sums_t[:, s * PART:(s + 1) * PART], fold[:, :],
                       start=True, stop=True)
                    last = mm(side_bank[1][:, at + LATENT:at + LATENT + 1], total[:, s * PART:(s + 1) * PART],
                              ones[:, :], start=True, stop=True)
                last.then_inc(sums_turned, 1)

            def concept_step(step, b1, j):
                n1 = b1 * BLOCKS + j
                if step == "enc":
                    pe.wait_ge(lat_low, n1 + 1 + FIRST)
                    mm(side_bank[0][0:64, :], w_to_high[:, :], lat_split[:, :], start=True, stop=False)
                    mm(side_bank[0][0:64, :], w_to_low[:, :], lat_split[:, :], start=False, stop=False)
                    mm(side_bank[0][0:64, :], fold_r[:, :], queries_flat[:, q_cols(b1, j)],
                       start=False, stop=True).then_inc(enc_ready, 1)
                if step == "max":
                    pe.wait_ge(enc_low, n1 + 1)
                    for i in range(2):
                        for h in range(2):
                            s = 2 * i + h
                            last = mm(side_bank[i][:, h * CONCEPTS:(h + 1) * CONCEPTS],
                                      cqueries[:, s * PART:(s + 1) * PART], ckeys_high[:, :], start=True, stop=True)
                        last.then_inc(cmax_ready, 1)
                if step == "shift":
                    pe.wait_ge(crow_max_ready, 2 * (n1 + 1))
                    for s in range(SUBS):
                        last = mm(side_bank[0][0:1, s * PART:(s + 1) * PART], crow_max[:, s:s + 1],
                                  neg_ident[:, :], start=True, stop=True)
                    last.then_inc(cshift_ready, 1)
                if step == "scores":
                    pe.wait_ge(cshift_taken, n1 + 1)
                    for t in range(CTILES):
                        mm(side_bank[1 - t][:, :], ckeys_high[:, t * PART:(t + 1) * PART], cqueries[:, :],
                           start=True, stop=False)
                        mm(side_bank[1 - t][:, :], ckeys_low[:, t * PART:(t + 1) * PART], cqueries_shift[:, :],
                           start=False, stop=True).then_inc(cscores_ready, 1)
                if step == "sums":
                    pe.wait_ge(cprobs_ready, CTILES * (n1 + 1))
                    for t in range(CTILES):
                        last = mm(side_bank[1][0:LATENT + 1, :], cvalues[:, t, :], cprobs[:, t, :],
                                  start=t == 0, stop=t == CTILES - 1)
                    last.then_inc(csums_ready, 1)
                if step == "turn":
                    pe.wait_ge(csums_copied, n1 + 1)
                    for s in range(SUBS):
                        last = nc.tensor.transpose(side_bank[0][:, s * (LATENT + 1):(s + 1) * (LATENT + 1)],
                                                   csums_t[:, s * PART:(s + 1) * PART],
                                                   ident[0:LATENT + 1, 0:LATENT + 1])
                    last.then_inc(csums_turned, 1)

            def output_step(step, n2):
                for k in (step, step + 1):
                    if k == 0:
                        pe.wait_ge(mix_low, n2 + 1 + FIRST)
                    if k >= 2:
                        pe.wait_ge(resid_added, KTILES * n2 + k - 1 + FIRST)
                    mm(side_bank[1 - k % 2][:, :], w_ot_high[:, k * PART:(k + 1) * PART], mix_split[:, :],
                       start=True, stop=False)
                    mm(side_bank[1 - k % 2][:, :], w_ot_low[:, k * PART:(k + 1) * PART], mix_split[:, :],
                       start=False, stop=True).then_inc(resid_ready, 1)

            def attend(b, j, parity, side, first=False, last=False):
                kb = b * BLOCKS + j
                if first:
                    for s in range(SUBS):
                        first_search(b, BLOCKS - 1, s)
                    turn_g(b, BLOCKS - 1)
                    shift_row(kb)
                    pe.wait_ge(low_ready, (b + 1) * BLOCKS + FIRST)
                    pe.wait_ge(shift_taken, kb + 1)
                    pe.wait_ge(values_ready, (b + 1) * BLOCKS + FIRST)
                    for t in range(LEAD):
                        if t >= 2:
                            pe.wait_ge(probs_high_ready, kb * KEYTILES + t - 1)
                        score(b, 0, t)
                done = 0
                for t in range(KEYTILES):
                    n = kb * KEYTILES + t
                    ahead = t + LEAD
                    if ahead < KEYTILES or not last:
                        if ahead == KEYTILES:
                            pe.wait_ge(shift_taken, kb + 2)
                        pe.wait_ge(probs_high_ready, n + LEAD - 1)
                        if ahead < KEYTILES:
                            score(b, j, ahead)
                        else:
                            score(b, j + 1, ahead - KEYTILES)
                    if not last:
                        if t == 0:
                            pe.wait_ge(search_q_loaded[1 - parity], 16 * (b * (BLOCKS // 2) + (j + 1) // 2 + 1))
                        for i in range(done, SEARCHED[t]):
                            search(kb + 1, 1 - parity, i)
                        done = SEARCHED[t]
                        if t == SHIFT_STEP:
                            shift_row(kb + 1)
                    if t == 0:
                        pe.wait_ge(sums_copied, kb + FIRST)
                    pe.wait_ge(probs_high_ready, n + 1)
                    mm(sum_bank[:, :], values[:, t, :], probs_high[:, t % NE, :], start=t == 0, stop=False)
                    pe.wait_ge(probs_low_ready, n + 1)
                    mm(sum_bank[:, :], values[:, t, :], probs_low[:, t % NL, :],
                       start=False, stop=t == KEYTILES - 1).then_inc(probs_used, 1)
                    if t == TURN_STEP - 1 and not first:
                        if side >= 2:
                            pe.wait_ge(resid_added, KTILES * (kb - 2 * BLOCKS) + FIRST)
                        turn(b, j - 1)
                    if side >= 1 and t in PE_CONCEPT:
                        if PE_CONCEPT[t] == "enc":
                            pe.wait_ge(clat_ready, kb - BLOCKS + FIRST)
                            if side >= 2:
                                pe.wait_ge(resid_added, KTILES * (kb - 2 * BLOCKS) + FIRST)
                        if PE_CONCEPT[t] == "max":
                            pe.wait_ge(lat_ready, kb + FIRST)
                        concept_step(PE_CONCEPT[t], b - 1, j)
                    if side >= 2 and t in PE_OUTPUT:
                        if PE_OUTPUT[t] == 0:
                            pe.wait_ge(clat_ready, kb - BLOCKS + 1 + FIRST)
                        output_step(PE_OUTPUT[t], kb - 2 * BLOCKS)

            def finish(b):
                if not isinstance(b, int) or b > 1:
                    pe.wait_ge(resid_added, KTILES * BLOCKS * (b - 1) + FIRST)
                turn(b, BLOCKS - 1)

            def tail(j, concept):
                n1 = (BATCH - 1) * BLOCKS + j
                n2 = (BATCH - 2 if concept else BATCH - 1) * BLOCKS + j
                pe.wait_ge(resid_added, KTILES * n2 + FIRST)
                if concept:
                    pe.wait_ge(lat_ready, BATCH * BLOCKS + FIRST)
                    pe.wait_ge(clat_ready, n1 + FIRST)
                    for step in ("enc", "max", "shift", "scores", "sums", "turn"):
                        concept_step(step, BATCH - 1, j)
                    pe.wait_ge(clat_ready, n1 + 1 + FIRST)
                for step in (0, 2):
                    output_step(step, n2)

            schedule(pe.Fori, project, attend, finish, tail)


TURN_STEP = 3
PE_CONCEPT = {8: "enc", 12: "max", 15: "shift", 18: "scores", 21: "sums", 24: "turn"}
ACT_CONCEPT = {4: "lat", 12: "enc", 19: "shift", 22: "probs", 25: "sums"}
DVE_CONCEPT = {10: "enc", 13: "max", 25: "normalize"}
POOL_CONCEPT = 5
PE_OUTPUT = {27: 0, 30: 2}
POOL_OUTPUT = {"mix": 9, "low": 14}
ACT_OUTPUT = 13
DVE_OUTPUT = {28: 0, 31: 2}


def kernel(x, L0_conv_concepts, L0_conv_w_theta, L0_conv_w_phi, L0_conv_w_g, L0_conv_w_o,
           L0_conv_gamma_sa, L0_conv_gamma_moca):
    import numpy as np
    import concourse.bacc as bacc
    from concourse import mybir
    from concourse.bass_utils import run_bass_kernel_spmd

    def by_partition(a):
        return np.ascontiguousarray(a.reshape(-1, PART, a.shape[1]).transpose(1, 0, 2))

    x = np.ascontiguousarray(x)
    theta, phi, g, w_o = (np.asarray(a) for a in (L0_conv_w_theta, L0_conv_w_phi, L0_conv_w_g, L0_conv_w_o))
    concepts = np.asarray(L0_conv_concepts)
    arrays = {
        "x": x.reshape(BATCH, CH, PIXELS),
        "w_thetaphi": by_partition(np.concatenate([theta, phi], axis=0).T),
        "w_g": by_partition(g.T),
        "w_o_t": np.ascontiguousarray(w_o.T),
        "w_o": by_partition(w_o),
        "concepts_t": np.ascontiguousarray(concepts.T),
        "concepts": by_partition(concepts),
        "gamma_sa": np.asarray(L0_conv_gamma_sa).reshape(1),
        "gamma_moca": np.asarray(L0_conv_gamma_moca).reshape(1),
        "consts": np.eye(PART, dtype=np.float32),
    }
    nc = bacc.Bacc("TRN2", target_bir_lowering=False, num_devices=1)
    args = {n: nc.dram_tensor(f"in_{n}", a.shape, mybir.dt.from_np(a.dtype), kind="ExternalInput").ap()
            for n, a in arrays.items()}
    out = nc.dram_tensor("out_0", (BATCH, CH, PIXELS), mybir.dt.float32, kind="ExternalOutput").ap()
    attention_kernel(nc, out=out, **args)
    r = run_bass_kernel_spmd(nc, [{f"in_{n}": a for n, a in arrays.items()}], core_ids=[0])
    return r.results[0]["out_0"].reshape(x.shape)
```

```python
import math

import concourse.bass as bass
from concourse import mybir
from contextlib import ExitStack

BATCH, CH, LATENT, CONCEPTS = 8, 512, 64, 256
PIXELS = 64 * 64
PART = 128
BLOCK = 512
BLOCKS = PIXELS // BLOCK
SUBS = BLOCK // PART
KTILES = CH // PART
KEYTILES = PIXELS // PART
CTILES = CONCEPTS // PART
XSLOTS = 2
NE = 4
NL = 2
XPOOL = 2
PAIRS = BLOCKS // 2
LEAD = 3

SEARCHES = BLOCKS * SUBS
SHIFT_STEP = 27
SEARCHED = [min(SEARCHES, -(-(t + 1) * SEARCHES // 26)) for t in range(KEYTILES)]
SETUP_STEPS = 6
FIRST = 1
SEARCH_BANKS = 4


class Lane:

    def __init__(self, name, sem, lat_in, lat_split, cqueries, cqueries_shift, crow_max, cprobs, csums_t, cinv,
                 clat_out, mix_in, mix_split, resid):
        self.lat_in, self.lat_split, self.cqueries, self.cqueries_shift = lat_in, lat_split, cqueries, cqueries_shift
        self.crow_max, self.cprobs, self.csums_t, self.cinv = crow_max, cprobs, csums_t, cinv
        self.clat_out, self.mix_in, self.mix_split, self.resid = clat_out, mix_in, mix_split, resid
        self.lat_loaded, self.mix_loaded = sem("lat_loaded" + name), sem("mix_loaded" + name)
        self.resid_loaded = sem("resid_loaded" + name)
        self.clat_stored, self.out_stored = sem("clat_stored" + name), sem("out_stored" + name)


def attention_kernel(nc, x, w_thetaphi, w_g, w_o_t, w_o, concepts_t, concepts, gamma_sa, gamma_moca, consts, out):
    fp32 = mybir.dt.float32
    fp32r = mybir.dt.float32r
    ALU = mybir.AluOpType
    ACT = mybir.ActivationFunctionType
    AX = mybir.AxisListType
    ds = bass.ds

    x_view = x.rearrange("b (k p) n -> b p k n", p=PART)
    out_view = out.rearrange("b (k p) n -> b p k n", p=PART)
    lat_dram = nc.dram_tensor("lat_scratch", (BATCH, PIXELS * LATENT), fp32).ap()
    clat_dram = nc.dram_tensor("clat_scratch", (BATCH, PIXELS * LATENT), fp32).ap()
    lat_store = lat_dram.rearrange("b (j s p c) -> b j p s c", j=BLOCKS, s=SUBS, p=PART)
    clat_store = clat_dram.rearrange("b (j s p c) -> b j p s c", j=BLOCKS, s=SUBS, p=PART)
    lat_load = lat_dram.rearrange("b (l n) -> b l n", l=LATENT)
    clat_load = clat_dram.rearrange("b (l n) -> b l n", l=LATENT)

    ctx = ExitStack()
    with ctx:
        def sb(name, shape, dt=fp32):
            return ctx.enter_context(nc.sbuf_tensor(name, shape, dt))

        def bank(name, shape=(PART, 512)):
            return ctx.enter_context(nc.psum_tensor(name, list(shape), fp32))

        def sem(name):
            return ctx.enter_context(nc.semaphore(name))

        ident = sb("ident", [PART, PART])
        neg_ident = sb("neg_ident", [PART, PART], fp32r)
        fold = sb("fold", [PART, LATENT])
        fold_r = sb("fold_r", [PART, LATENT], fp32r)
        ones = sb("ones", [PART, 1])
        gamma = sb("gamma", [PART, 2])
        w_tp_high = sb("w_tp_high", [PART, KTILES, PART], fp32r)
        w_tp_low = sb("w_tp_low", [PART, KTILES, PART], fp32r)
        w_g_split = sb("w_g_split", [PART, KTILES, PART], fp32r)
        w_ot_high = sb("w_ot_high", [PART, CH], fp32r)
        w_ot_low = sb("w_ot_low", [PART, CH], fp32r)
        w_to_high = sb("w_to_high", [PART, LATENT], fp32r)
        w_to_low = sb("w_to_low", [PART, LATENT], fp32r)
        ckeys_high = sb("ckeys_high", [PART, CONCEPTS], fp32r)
        ckeys_low = sb("ckeys_low", [PART, CONCEPTS], fp32r)
        cvalues = sb("cvalues", [PART, CTILES, LATENT + 1])

        x_in = sb("x_in", [PART, XSLOTS, KTILES, BLOCK])
        x_high = sb("x_high", [PART, XSLOTS, KTILES, BLOCK], fp32r)
        x_low = sb("x_low", [PART, KTILES, BLOCK], fp32r)
        queries = sb("queries", [PART, 2, PIXELS], fp32r)
        queries_shift = sb("queries_shift", [PART, PIXELS], fp32r)
        keys_high = sb("keys_high", [PART, PIXELS], fp32r)
        keys_low = sb("keys_low", [PART, PIXELS], fp32r)
        values = sb("values", [PART, KEYTILES, PART], fp32r)
        search_q = sb("search_q", [PART, 2, BLOCK], fp32r)
        tile_max = sb("tile_max", [PART, SUBS, BLOCKS])
        row_max = sb("row_max", [PART, SUBS], fp32r)
        probs = sb("probs", [PART, NE, BLOCK])
        probs_high = sb("probs_high", [PART, NE, BLOCK], fp32r)
        probs_low = sb("probs_low", [PART, NL, BLOCK], fp32r)
        total = sb("total", [PART, BLOCK])
        g_parts = total
        sums_t = sb("sums_t", [PART, BLOCK])
        inv = sb("inv", [PART, SUBS])
        lat_out = sb("lat_out", [PART, SUBS, LATENT])

        lat_in = sb("lat_in", [PART, BLOCK])
        lat_split = sb("lat_split", [PART, BLOCK], fp32r)
        cqueries = sb("cqueries", [PART, BLOCK], fp32r)
        cqueries_shift = sb("cqueries_shift", [PART, BLOCK], fp32r)
        crow_max = sb("crow_max", [PART, SUBS], fp32r)
        cprobs = sb("cprobs", [PART, CTILES, BLOCK])
        csums_t = sums_t[0:LATENT + 1, :]
        cinv = sb("cinv", [PART, SUBS])
        clat_out = sb("clat_out", [PART, SUBS, LATENT])

        mix_in = sb("mix_in", [PART, 2, BLOCK])
        mix_split = sb("mix_split", [PART, BLOCK], fp32r)
        resid = sb("resid", [PART, KTILES, BLOCK])
        raw_tp = resid[:, 0, :].rearrange("p (k c) -> p k c", k=KTILES)
        raw_g = resid[:, 1, 0:KTILES * LATENT].rearrange("p (k c) -> p k c", k=KTILES)
        raw_o = resid[:, 1, KTILES * LATENT:].rearrange("p (k c) -> p k c", k=KTILES)
        raw_ot = resid[:, 2, :]
        raw_ct = resid[:, 3, 0:CONCEPTS]

        score_bank = [bank(f"score_bank{i}") for i in range(2)]
        max_bank = [bank(f"max_bank{i}") for i in range(2)]
        sum_bank = bank("sum_bank")
        total_bank = bank("total_bank")
        side_bank = [bank(f"side_bank{i}") for i in range(2)]
        first_search_bank = max_bank + [sum_bank, total_bank]

        consts_in, weights_in = sem("consts_in"), sem("weights_in")
        x_loaded = [sem(f"x_loaded{i}") for i in range(XSLOTS)]
        search_q_loaded = [sem(f"search_q_loaded{i}") for i in range(2)]
        lat_stored = sem("lat_stored")
        setup_dve, setup_pe, setup_ready = sem("setup_dve"), sem("setup_pe"), sem("setup_ready")
        x_high_ready, x_low_pool, x_low_dve = sem("x_high_ready"), sem("x_low_pool"), sem("x_low_dve")
        thetaphi_ready, g_ready, g_copied = sem("thetaphi_ready"), sem("g_ready"), sem("g_copied")
        g_turned, values_high_ready, values_ready = sem("g_turned"), sem("values_high_ready"), sem("values_ready")
        high_ready, low_ready = sem("high_ready"), sem("low_ready")
        max_ready, max_taken = sem("max_ready"), sem("max_taken")
        row_max_ready, shift_ready, shift_taken = sem("row_max_ready"), sem("shift_ready"), sem("shift_taken")
        scores_ready, probs_ready, probs_high_ready = sem("scores_ready"), sem("probs_ready"), sem("probs_high_ready")
        probs_low_ready, probs_added, probs_used = sem("probs_low_ready"), sem("probs_added"), sem("probs_used")
        sums_copied, sums_turned = sem("sums_copied"), sem("sums_turned")
        inv_ready, lat_ready = sem("inv_ready"), sem("lat_ready")
        lat_high, lat_low = sem("lat_high"), sem("lat_low")
        enc_ready, enc_high, enc_low = sem("enc_ready"), sem("enc_high"), sem("enc_low")
        cmax_ready, crow_max_ready = sem("cmax_ready"), sem("crow_max_ready")
        cshift_ready, cshift_taken = sem("cshift_ready"), sem("cshift_taken")
        cscores_ready, cprobs_ready = sem("cscores_ready"), sem("cprobs_ready")
        csums_ready, csums_copied, csums_turned = sem("csums_ready"), sem("csums_copied"), sem("csums_turned")
        cinv_ready, clat_ready = sem("cinv_ready"), sem("clat_ready")
        mix_added, mix_high, mix_low = sem("mix_added"), sem("mix_high"), sem("mix_low")
        resid_ready, resid_added = sem("resid_ready"), sem("resid_added")

        raw = lambda ap: ap.bitcast(fp32)

        def block_cols(j):
            return ds(j * BLOCK, BLOCK) if not isinstance(j, int) else slice(j * BLOCK, (j + 1) * BLOCK)

        def q_cols(b, j):
            at = (b % 2) * PIXELS + j * BLOCK
            return ds(at, BLOCK) if not isinstance(at, int) else slice(at, at + BLOCK)

        queries_flat = queries[:, :, :].rearrange("p a n -> p (a n)")

        lanes = [
            Lane("0", sem, lat_in=lat_in, lat_split=lat_split, cqueries=cqueries, cqueries_shift=cqueries_shift,
                 crow_max=crow_max, cprobs=cprobs, csums_t=csums_t, cinv=cinv, clat_out=clat_out,
                 mix_in=mix_in, mix_split=mix_split, resid=resid),
            Lane("1", sem, lat_in=x_in[:, 0, 0, :], lat_split=x_high[:, 0, 0, :], cqueries=x_high[:, 0, 1, :],
                 cqueries_shift=x_high[:, 0, 2, :], crow_max=row_max, cprobs=x_in[:, 0, 1:3, :],
                 csums_t=x_in[0:LATENT + 1, 0, 3, :], cinv=inv, clat_out=lat_out,
                 mix_in=x_in[:, 1, 0:2, :], mix_split=x_high[:, 0, 3, :], resid=probs)]
        tail_banks = [side_bank, max_bank]
        tail_out_banks = [score_bank, [sum_bank, total_bank]]

        g_by_key = side_bank[1][:, 0:SUBS * LATENT].rearrange("p (s c) -> p s c", s=SUBS)

        def tiles_of(j):
            return slice(j * SUBS, (j + 1) * SUBS) if isinstance(j, int) else ds(j * SUBS, SUBS)

        def x_count(b, j):
            return 16 * (b * (BLOCKS // XSLOTS) + j // XSLOTS + 1)

        def schedule(loop, project, attend, finish, tail):
            def batch(b, side):
                project(b, 0, 0)
                with loop(0, (BLOCKS - 4) // 2) as pair:
                    project(b, 2 * pair + 1, 1)
                    project(b, 2 * pair + 2, 0)
                for j in range(BLOCKS - 3, BLOCKS):
                    project(b, j, j % 2)
                attend(b, 0, 0, side, first=True)
                with loop(0, (BLOCKS - 2) // 2) as pair:
                    attend(b, 2 * pair + 1, 1, side)
                    attend(b, 2 * pair + 2, 0, side)
                attend(b, BLOCKS - 1, 1, side, last=True)

            batch(0, 0)
            batch(1, 1)
            with loop(2, BATCH - 1) as b:
                batch(b, 2)
            batch(BATCH - 1, 2)
            finish(BATCH - 1)
            for concept in (True, False):
                with loop(0, PAIRS) as pair:
                    tail(pair, concept)

        def tail_blocks(pair, concept):
            for i, lane in enumerate(lanes):
                j = 2 * pair + i
                n2 = (BATCH - 2 if concept else BATCH - 1) * BLOCKS + j
                had1 = (0 if i else (BATCH - 1) * BLOCKS) + pair
                had2 = (0 if i else (BATCH - 2) * BLOCKS) + (0 if concept else PAIRS) + pair
                yield lane, j, (BATCH - 1) * BLOCKS + j, n2, had1, had2

        def splits_ahead(b, j):
            return not (is_last(b) and isinstance(j, int) and j >= BLOCKS - XSLOTS)

        def has_next(b, j):
            return not (is_last(b) and isinstance(j, int) and j == BLOCKS - 1)

        def is_last(b):
            return isinstance(b, int) and b == BATCH - 1

        block = ctx.enter_context(nc.Block())

        @block.sync
        def _(sp):
            def load_x(b, j, slot):
                src = x_view[ds(b, 1), :, :, block_cols(j)].rearrange("a p k n -> (a p) k n")
                sp.dma_start(x_in[:, slot, :, :], src).then_inc(x_loaded[slot], 16)

            def load_search_q(b, j, parity):
                sp.dma_start(raw(search_q[:, parity, :]), raw(queries_flat[:, q_cols(b, j)]))\
                  .then_inc(search_q_loaded[parity], 16)

            sp.dma_start(ident[:, :], consts).then_inc(consts_in, 16)

            def counted(value):
                return value if isinstance(value, int) else sp.snap(value)

            def load_x_ahead(b, j):
                if splits_ahead(b, j):
                    split = counted(b * BLOCKS + j + 1)
                    sp.wait_ge(x_low_pool, split)
                    sp.wait_ge(x_low_dve, split)
                    load_x(b + (j + XSLOTS) // BLOCKS, (j + XSLOTS) % BLOCKS, j % XSLOTS)

            def project(b):
                for j in range(BLOCKS):
                    if j > 0:
                        load_x_ahead(b, j)
                    if j < 2:
                        sp.wait_ge(low_ready, b * BLOCKS + j + 1 + FIRST)
                        load_search_q(b, j, j)

            def load_lat(b1, j, lane, split):
                sp.wait_ge(lat_low, split)
                src = lat_load[ds(b1, 1), :, block_cols(j)].rearrange("a l n -> (a l) n")
                sp.dma_start(lane.lat_in[0:64, :], src).then_inc(lane.lat_loaded, 16)
                sp.dma_start(lane.lat_in[64:128, :], src).then_inc(lane.lat_loaded, 16)

            def load_mix(b2, j, lane, split):
                sp.wait_ge(mix_low, split)
                for half in (0, 64):
                    for i, view in enumerate((lat_load, clat_load)):
                        src = view[ds(b2, 1), :, block_cols(j)].rearrange("a l n -> (a l) n")
                        sp.dma_start(lane.mix_in[half:half + 64, i, :], src).then_inc(lane.mix_loaded, 16)

            def load_resid(b2, j, lane, had):
                sp.wait_ge(lane.out_stored, 16 * had + FIRST)
                src = x_view[ds(b2, 1), :, :, block_cols(j)].rearrange("a p k n -> (a p) k n")
                sp.dma_start(lane.resid[:, :, :], src).then_inc(lane.resid_loaded, 16)

            def load_side(b, j, side):
                if side >= 1:
                    n1 = counted((b - 1) * BLOCKS + j + FIRST)
                    if j == 0:
                        sp.wait_ge(lat_stored, 16 * BLOCKS * b + FIRST)
                    load_lat(b - 1, j, lanes[0], n1)
                if side >= 2:
                    n2 = counted((b - 2) * BLOCKS + j + FIRST)
                    if j == 0:
                        sp.wait_ge(lanes[0].clat_stored, 16 * BLOCKS * (b - 1) + FIRST)
                    load_mix(b - 2, j, lanes[0], n2)

            def store_lat(b, j):
                sp.wait_ge(lat_ready, b * BLOCKS + j + 1 + FIRST)
                dst = lat_store[ds(b, 1), ds(j, 1), :, :, :].rearrange("a j p s c -> (a j p) s c")
                sp.dma_start(dst, lat_out[:, :, :]).then_inc(lat_stored, 16)

            def store_clat(b1, j, lane=lanes[0]):
                sp.wait_ge(clat_ready, b1 * BLOCKS + j + 1 + FIRST)
                dst = clat_store[ds(b1, 1), ds(j, 1), :, :, :].rearrange("a j p s c -> (a j p) s c")
                sp.dma_start(dst, lane.clat_out[:, :, :]).then_inc(lane.clat_stored, 16)

            def store_out(b2, j, lane=lanes[0]):
                sp.wait_ge(resid_added, KTILES * (b2 * BLOCKS + j + 1) + FIRST)
                dst = out_view[ds(b2, 1), :, :, block_cols(j)].rearrange("a p k n -> (a p) k n")
                sp.dma_start(dst, lane.resid[:, :, :]).then_inc(lane.out_stored, 16)

            def load_next(b, j):
                sp.wait_ge(max_ready, (b * BLOCKS + j + 1) * SEARCHES)
                load_search_q(b, j + 2, j % 2)

            def attend(b, j, side):
                if j == 0:
                    load_side(b, j, side)
                if side >= 2:
                    load_resid(b - 2, j, lanes[0], counted((b - 2) * BLOCKS + j))
                if j > 0:
                    store_lat(b, j - 1)
                if j < BLOCKS - 1:
                    load_side(b, j + 1, side)
                if j < BLOCKS - 2:
                    load_next(b, j)
                if side >= 1:
                    store_clat(b - 1, j)
                if side >= 2:
                    store_out(b - 2, j)

            def batch(b, side):
                project(b)
                for j in range(BLOCKS):
                    attend(b, j, side)
                if not is_last(b):
                    load_x_ahead(b + 1, 0)
                store_lat(b, BLOCKS - 1)

            for u in range(XSLOTS):
                load_x(0, u, u)
            for dst, src in ((raw_tp[:, :, :], w_thetaphi), (raw_g[:, :, :], w_g), (raw_o[:, :, :], w_o),
                             (cvalues[:, :, 0:LATENT], concepts),
                             (raw_ot[0:64, :], w_o_t), (raw_ot[64:128, :], w_o_t),
                             (raw_ct[0:64, :], concepts_t), (raw_ct[64:128, :], concepts_t),
                             (gamma[:, 0:1], gamma_sa.partition_broadcast(PART)),
                             (gamma[:, 1:2], gamma_moca.partition_broadcast(PART))):
                sp.dma_start(dst, src).then_inc(weights_in, 16)
            load_x_ahead(0, 0)
            batch(0, 0)
            batch(1, 1)
            with sp.Fori(2, BATCH - 1) as b:
                batch(b, 2)
            batch(BATCH - 1, 2)
            def tail_loads(pair, concept):
                for lane, j, n1, n2, had1, had2 in tail_blocks(pair, concept):
                    if concept:
                        load_lat(BATCH - 1, j, lane, n1 - j % 2 + FIRST)
                    load_mix(BATCH - 2 if concept else BATCH - 1, j, lane, n2 - j % 2 + FIRST)

            sp.wait_ge(lat_stored, 16 * BLOCKS * BATCH + FIRST)
            sp.wait_ge(lanes[0].clat_stored, 16 * BLOCKS * (BATCH - 1) + FIRST)
            for concept in (True, False):
                b2 = BATCH - 2 if concept else BATCH - 1
                tail_loads(0, concept)
                for pair in range(PAIRS):
                    for lane, j, n1, n2, had1, had2 in tail_blocks(pair, concept):
                        load_resid(b2, j, lane, had2)
                    if pair < PAIRS - 1:
                        tail_loads(pair + 1, concept)
                    for lane, j, n1, n2, had1, had2 in tail_blocks(pair, concept):
                        store_out(b2, j, lane)
                    if concept:
                        for lane, j, n1, n2, had1, had2 in tail_blocks(pair, concept):
                            store_clat(BATCH - 1, j, lane)
                sp.wait_ge(lanes[0].clat_stored, 16 * ((BATCH - 1) * BLOCKS + PAIRS) + FIRST)
                sp.wait_ge(lanes[1].clat_stored, 16 * PAIRS + FIRST)
            sp.wait_ge(lanes[0].out_stored, 16 * ((BATCH - 2) * BLOCKS + 2 * PAIRS) + FIRST)
            sp.wait_ge(lanes[1].out_stored, 16 * 2 * PAIRS + FIRST)

        @block.gpsimd
        def _(pool):
            def split_x(kb, slot):
                pool.wait_ge(x_high_ready, kb + 1)
                nc.gpsimd.tensor_tensor(x_low[:, 0:XPOOL, :], x_in[:, slot, 0:XPOOL, :],
                                        raw(x_high[:, slot, 0:XPOOL, :]), ALU.subtract).then_inc(x_low_pool, 1)

            def project(b, j, parity):
                if has_next(b, j):
                    pool.wait_ge(g_ready, b * BLOCKS + j + 1)
                    split_x(b * BLOCKS + j + 1, 1 - parity)

            def split_probs(b, j, t):
                n = (b * BLOCKS + j) * KEYTILES + t
                pool.wait_ge(probs_high_ready, n + 1)
                if not (isinstance(n, int) and n < NL):
                    pool.wait_ge(probs_used, n - NL + 1)
                nc.gpsimd.tensor_tensor(probs_low[:, t % NL, :], probs[:, t % NE, :],
                                        raw(probs_high[:, t % NE, :]), ALU.subtract).then_inc(probs_low_ready, 1)

            def lat_step(n1, lane=lanes[0]):
                pool.wait_ge(lat_high, n1 + 1)
                nc.gpsimd.tensor_tensor(lane.lat_split[64:128, :], lane.lat_in[64:128, :],
                                        raw(lane.lat_split[64:128, :]), ALU.subtract).then_inc(lat_low, 1)

            def mix_step(n2, had, lane=lanes[0]):
                pool.wait_ge(lane.mix_loaded, 64 * (had + 1))
                nc.gpsimd.tensor_tensor(lane.mix_in[:, 0, :], lane.mix_in[:, 0, :], lane.mix_in[:, 1, :], ALU.add)\
                    .then_inc(mix_added, 1)

            def mix_low_step(n2, lane=lanes[0]):
                pool.wait_ge(mix_high, n2 + 1)
                nc.gpsimd.tensor_tensor(lane.mix_split[64:128, :], lane.mix_in[64:128, 0, :],
                                        raw(lane.mix_split[64:128, :]), ALU.subtract).then_inc(mix_low, 1)

            def attend(b, j, parity, side, first=False, last=False):
                n = b * BLOCKS + j
                for t in range(KEYTILES):
                    split_probs(b, j, t)
                    if side >= 1 and t == POOL_CONCEPT:
                        pool.wait_ge(probs_low_ready, n * KEYTILES + t + 1)
                        lat_step(n - BLOCKS)
                        pool.wait_ge(lat_low, n - BLOCKS + 1 + FIRST)
                    if side >= 2 and t == POOL_OUTPUT["mix"]:
                        mix_step(n - 2 * BLOCKS, n - 2 * BLOCKS)
                    if side >= 2 and t == POOL_OUTPUT["low"]:
                        pool.wait_ge(probs_low_ready, n * KEYTILES + t + 1)
                        mix_low_step(n - 2 * BLOCKS)
                        pool.wait_ge(mix_low, n - 2 * BLOCKS + 1 + FIRST)

            def tail(pair, concept):
                blocks = list(tail_blocks(pair, concept))
                pool.wait_ge(mix_low, blocks[0][3] + FIRST)
                if concept:
                    for lane, j, n1, n2, had1, had2 in blocks:
                        lat_step(n1, lane)
                        pool.wait_ge(lat_low, n1 + 1 + FIRST)
                for lane, j, n1, n2, had1, had2 in blocks:
                    mix_step(n2, had2, lane)
                pool.wait_ge(mix_added, blocks[1][3] + 1)
                for lane, j, n1, n2, had1, had2 in blocks:
                    mix_low_step(n2, lane)
                    pool.wait_ge(mix_low, n2 + 1 + FIRST)

            split_x(0, 0)
            schedule(pool.Fori, project, attend, lambda b: None, tail)

        @block.scalar
        def _(act):
            def split_x(kb, slot):
                act.wait_ge(x_loaded[slot], 16 * (kb // XSLOTS + 1))
                nc.scalar.activation(x_high[:, slot, :, :], x_in[:, slot, :, :], ACT.Copy).then_inc(x_high_ready, 1)

            def copy_values(b, j):
                kb = b * BLOCKS + j
                act.wait_ge(g_turned, kb + 1)
                nc.scalar.activation(values[:, tiles_of(j), 0:LATENT], g_by_key, ACT.Copy)\
                    .then_inc(values_high_ready, 1)

            def project(b, j, parity):
                kb = b * BLOCKS + j
                if not (isinstance(j, int) and j == 0):
                    copy_values(b, j - 1)
                elif not (isinstance(b, int) and b == 0):
                    copy_sums(b - 1, BLOCKS - 1)
                tp = score_bank[parity]
                act.wait_ge(thetaphi_ready, kb + 1)
                nc.scalar.activation(keys_high[0:64, block_cols(j)], tp[64:128, :], ACT.Copy)
                nc.scalar.activation(keys_high[64:128, block_cols(j)], tp[64:128, :], ACT.Copy)
                nc.scalar.activation(queries_flat[0:64, q_cols(b, j)], tp[0:64, :], ACT.Copy)
                nc.scalar.activation(queries_shift[0:64, block_cols(j)], tp[0:64, :], ACT.Copy)\
                    .then_inc(high_ready, 1)
                act.wait_ge(g_ready, kb + 1)
                if not (isinstance(kb, int) and kb == 0):
                    act.wait_ge(g_turned, kb)
                nc.scalar.activation(g_parts[:, :], side_bank[0][:, :], ACT.Copy).then_inc(g_copied, 1)
                if splits_ahead(b, j):
                    act.wait_ge(x_loaded[parity], x_count(b, j + XSLOTS))
                    nc.scalar.activation(x_high[:, parity, :, :], x_in[:, parity, :, :], ACT.Copy)\
                        .then_inc(x_high_ready, 1)

            def copy_sums(b, j):
                kb = b * BLOCKS + j
                act.wait_ge(probs_used, (kb + 1) * KEYTILES)
                act.wait_ge(sums_turned, kb + FIRST)
                nc.scalar.activation(sums_t[:, :], sum_bank[:, :], ACT.Copy).then_inc(sums_copied, 1)

            def copy_shift(b, j):
                act.wait_ge(shift_ready, b * BLOCKS + j + 1)
                nc.scalar.activation(queries_shift[64:65, block_cols(j)], max_bank[0][0:1, :], ACT.Copy)\
                    .then_inc(shift_taken, 1)

            def exp_scores(b, j, t):
                n = (b * BLOCKS + j) * KEYTILES + t
                started = not (isinstance(n, int) and n < NE)
                act.wait_ge(scores_ready, n + 1)
                if started:
                    act.wait_ge(probs_low_ready, n - NE + 1)
                    act.wait_ge(probs_added, n - NE + 1)
                nc.scalar.activation(probs[:, t % NE, :], score_bank[t % 2][:, :], ACT.Exp).then_inc(probs_ready, 1)
                if started:
                    act.wait_ge(probs_used, n - NE + 1)
                nc.scalar.activation(probs_high[:, t % NE, :], score_bank[t % 2][:, :], ACT.Exp)\
                    .then_inc(probs_high_ready, 1)

            def concept_step(step, n1, had, lane=lanes[0], banks=side_bank):
                if step == "lat":
                    act.wait_ge(lane.lat_loaded, 32 * (had + 1))
                    nc.scalar.activation(lane.lat_split[:, :], lane.lat_in[:, :], ACT.Copy).then_inc(lat_high, 1)
                if step == "enc":
                    act.wait_ge(enc_ready, n1 + 1)
                    nc.scalar.activation(lane.cqueries[0:64, :], banks[0][0:64, :], ACT.Copy)
                    nc.scalar.activation(lane.cqueries_shift[0:64, :], banks[0][0:64, :], ACT.Copy)\
                        .then_inc(enc_high, 1)
                if step == "shift":
                    act.wait_ge(cshift_ready, n1 + 1)
                    nc.scalar.activation(lane.cqueries_shift[64:65, :], banks[0][0:1, :], ACT.Copy)\
                        .then_inc(cshift_taken, 1)
                if step == "probs":
                    for t in range(CTILES):
                        act.wait_ge(cscores_ready, CTILES * n1 + t + 1)
                        nc.scalar.activation(lane.cprobs[:, t, :], banks[1 - t][:, :], ACT.Exp)\
                            .then_inc(cprobs_ready, 1)
                if step == "sums":
                    act.wait_ge(csums_ready, CTILES * (n1 + 1))
                    nc.scalar.activation(lane.csums_t[:, :], banks[1][0:LATENT + 1, :], ACT.Copy)\
                        .then_inc(csums_copied, 1)

            def output_step(n2, lane=lanes[0]):
                act.wait_ge(mix_added, n2 + 1)
                nc.scalar.activation(lane.mix_split[:, :], lane.mix_in[:, 0, :], ACT.Copy).then_inc(mix_high, 1)

            def attend(b, j, parity, side, first=False, last=False):
                n = b * BLOCKS + j
                if first:
                    copy_values(b, BLOCKS - 1)
                    copy_shift(b, 0)
                for t in range(KEYTILES):
                    if t == LEAD - 1 and not first:
                        copy_sums(b, j - 1)
                    exp_scores(b, j, t)
                    if t == SHIFT_STEP + LEAD - 1 and not last:
                        copy_shift(b, j + 1)
                    if side >= 1 and t in ACT_CONCEPT:
                        concept_step(ACT_CONCEPT[t], n - BLOCKS, n - BLOCKS)
                    if side >= 2 and t == ACT_OUTPUT:
                        output_step(n - 2 * BLOCKS)

            def tail(pair, concept):
                blocks = list(tail_blocks(pair, concept))

                def concept_steps(step):
                    for i, (lane, j, n1, n2, had1, had2) in enumerate(blocks):
                        concept_step(step, n1, had1, lane, tail_banks[i])

                if concept:
                    act.wait_ge(enc_ready, blocks[0][2])
                    concept_steps("lat")
                    concept_steps("enc")
                act.wait_ge(resid_ready, KTILES * blocks[0][3])
                for lane, j, n1, n2, had1, had2 in blocks:
                    output_step(n2, lane)
                if concept:
                    for step in ("shift", "probs", "sums"):
                        concept_steps(step)

            for u in range(XSLOTS):
                split_x(u, u)
            schedule(act.Fori, project, attend, lambda b: copy_sums(b, BLOCKS - 1), tail)

        @block.vector
        def _(dve):
            steps = [0]

            def then(ins):
                steps[0] += 1
                ins.then_inc(setup_dve, 1)
                dve.wait_ge(setup_dve, steps[0])

            def split_x(kb, slot):
                dve.wait_ge(x_high_ready, kb + 1)
                nc.vector.tensor_tensor(x_low[:, XPOOL:KTILES, :], x_in[:, slot, XPOOL:KTILES, :],
                                        raw(x_high[:, slot, XPOOL:KTILES, :]), ALU.subtract).then_inc(x_low_dve, 1)

            gain = float(1.0 / math.sqrt(CH))
            out_gain = float(1.0 / math.sqrt(LATENT))
            released = (lat_ready, lat_stored, clat_ready, lanes[0].clat_stored, lanes[0].out_stored, lat_low, mix_low,
                        resid_added, sums_copied, sums_turned, low_ready, values_ready)
            released += (lanes[1].clat_stored, lanes[1].out_stored)
            for i, buffer in enumerate(released):
                nc.vector.memset(tile_max[:, i // BLOCKS, i % BLOCKS:i % BLOCKS + 1], 0.0).then_inc(buffer, FIRST)
            nc.vector.memset(tile_max[:, SUBS - 1, :], 0.0).then_inc(max_taken, SEARCH_BANKS)
            nc.vector.memset(raw(keys_low[64:128, :]), 0.0)
            nc.vector.memset(raw(queries_shift[64:128, :]), 0.0)
            nc.vector.memset(raw(ckeys_low[64:128, :]), 0.0)
            nc.vector.memset(raw(cqueries_shift[64:128, :]), 0.0)
            nc.vector.memset(ones[:, :], 1.0)
            then(nc.vector.memset(cvalues[:, :, LATENT:LATENT + 1], 1.0))
            nc.vector.memset(raw(keys_low[64:65, :]), 1.0)
            then(nc.vector.memset(raw(ckeys_low[64:65, :]), 1.0))
            split_x(0, 0)
            dve.wait_ge(consts_in, 16)
            nc.vector.tensor_scalar(neg_ident[:, :], ident[:, :], -1.0, None, ALU.mult)
            for half in (0, 64):
                for folded in (fold, fold_r):
                    nc.vector.tensor_copy(folded[half:half + 64, :], ident[half:half + 64, half:half + 64])
            dve.wait_ge(weights_in, 16 * 10)
            nc.vector.tensor_scalar(raw_tp[:, :, :], raw_tp[:, :, :], gain, None, ALU.mult)
            nc.vector.tensor_scalar(raw_g[:, :, :], raw_g[:, :, :], gain, None, ALU.mult)
            nc.vector.tensor_scalar(raw_o[:, :, :], raw_o[:, :, :], out_gain, None, ALU.mult)
            nc.vector.tensor_scalar(raw_ot[:, :], raw_ot[:, :], out_gain, None, ALU.mult)
            nc.vector.tensor_scalar(cvalues[:, :, 0:LATENT], cvalues[:, :, 0:LATENT], gamma[:, 1:2], None, ALU.mult)
            then(nc.vector.tensor_copy(ckeys_high[:, :], raw_ct[:, :]))
            nc.vector.tensor_scalar(raw_g[:, :, :], raw_g[:, :, :], gamma[:, 0:1], None, ALU.mult)
            nc.vector.tensor_copy(w_tp_high[:, :, :], raw_tp[:, :, :])
            then(nc.vector.tensor_copy(w_ot_high[:, :], raw_ot[:, :]))
            nc.vector.tensor_tensor(w_tp_low[:, :, :], raw_tp[:, :, :], raw(w_tp_high[:, :, :]), ALU.subtract)
            nc.vector.tensor_copy(w_g_split[:, :, 0:LATENT], raw_g[:, :, :])
            nc.vector.tensor_tensor(w_ot_low[:, :], raw_ot[:, :], raw(w_ot_high[:, :]), ALU.subtract)
            then(nc.vector.tensor_tensor(ckeys_low[0:64, :], raw_ct[0:64, :], raw(ckeys_high[0:64, :]), ALU.subtract))
            then(nc.vector.tensor_tensor(w_g_split[:, :, LATENT:PART], raw_g[:, :, :],
                                         raw(w_g_split[:, :, 0:LATENT]), ALU.subtract))
            assert steps[0] == SETUP_STEPS
            dve.wait_ge(setup_pe, 1)
            product = side_bank[0][0:64, 0:LATENT]
            nc.vector.tensor_copy(w_to_high[0:64, :], product)
            then(nc.vector.tensor_copy(w_to_high[64:128, :], product))
            nc.vector.tensor_tensor(w_to_low[0:64, :], product, raw(w_to_high[0:64, :]), ALU.subtract)
            nc.vector.tensor_tensor(w_to_low[64:128, :], product, raw(w_to_high[0:64, :]), ALU.subtract)\
                .then_inc(setup_ready, 1)

            def take_max(entry, out, searched):
                dve.wait_ge(max_ready, entry + 1)
                nc.vector.reduce_max(out, searched[:, :], AX.X).then_inc(max_taken, 1)

            def finish_max(kb):
                dve.wait_ge(max_taken, (kb + 1) * SEARCHES + SEARCH_BANKS)
                nc.vector.tensor_reduce(row_max[:, :], tile_max[:, :, :], AX.X, ALU.max).then_inc(row_max_ready, 1)

            def first_search(b, j):
                for s in range(SUBS):
                    at = slice(j, j + 1) if isinstance(j, int) else ds(j, 1)
                    take_max(b * BLOCKS * SEARCHES + j * SUBS + s, tile_max[:, s, at], first_search_bank[s])

            def low_values(b, j):
                kb = b * BLOCKS + j
                dve.wait_ge(values_high_ready, kb + 1)
                nc.vector.tensor_tensor(values[:, tiles_of(j), LATENT:PART], g_by_key,
                                        raw(values[:, tiles_of(j), 0:LATENT]), ALU.subtract)\
                    .then_inc(values_ready, 1)

            def project(b, j, parity):
                kb = b * BLOCKS + j
                tp = score_bank[parity]
                if not (isinstance(j, int) and j == 0):
                    first_search(b, j - 1)
                    low_values(b, j - 1)
                elif not (isinstance(b, int) and b == 0):
                    normalize(b - 1, BLOCKS - 1)
                dve.wait_ge(high_ready, kb + 1)
                nc.vector.tensor_tensor(queries_flat[64:128, q_cols(b, j)], tp[0:64, :],
                                        raw(queries_flat[0:64, q_cols(b, j)]), ALU.subtract)
                nc.vector.tensor_tensor(keys_low[0:64, block_cols(j)], tp[64:128, :],
                                        raw(keys_high[64:128, block_cols(j)]), ALU.subtract).then_inc(low_ready, 1)
                if has_next(b, j):
                    dve.wait_ge(g_ready, kb + 1)
                    split_x(kb + 1, 1 - parity)

            def add_probs(b, j, t):
                kb = b * BLOCKS + j
                n = kb * KEYTILES + t
                if t == 0:
                    return
                dve.wait_ge(probs_ready, n + 1)
                if t == 1:
                    if not (isinstance(kb, int) and kb == 0):
                        dve.wait_ge(probs_added, kb * KEYTILES)
                    nc.vector.tensor_tensor(total_bank[:, :], probs[:, 0, :], probs[:, 1, :], ALU.add)\
                        .then_inc(probs_added, 2)
                    return
                dve.wait_ge(probs_added, n)
                if t == KEYTILES - 1:
                    dve.wait_ge(sums_turned, kb + FIRST)
                nc.vector.tensor_tensor(total[:, :] if t == KEYTILES - 1 else total_bank[:, :], total_bank[:, :],
                                        probs[:, t % NE, :], ALU.add).then_inc(probs_added, 1)

            def normalize(b, j):
                kb = b * BLOCKS + j
                turned = side_bank[1][:, 0:SUBS * (LATENT + 1)].rearrange("p (s c) -> p s c", s=SUBS)
                dve.wait_ge(sums_turned, kb + 1 + FIRST)
                nc.vector.reciprocal(inv[:, :], turned[:, :, LATENT]).then_inc(inv_ready, 1)
                dve.wait_ge(inv_ready, kb + 1)
                dve.wait_ge(lat_stored, 16 * kb + FIRST)
                nc.vector.tensor_tensor(lat_out[:, :, :], turned[:, :, 0:LATENT],
                                        inv[:, :].unsqueeze(2).to_broadcast([PART, SUBS, LATENT]), ALU.mult)\
                    .then_inc(lat_ready, 1)

            def concept_step(step, n1, had, lane=lanes[0], banks=side_bank):
                if step == "enc":
                    dve.wait_ge(enc_high, n1 + 1)
                    nc.vector.tensor_tensor(lane.cqueries[64:128, :], banks[0][0:64, :],
                                            raw(lane.cqueries[0:64, :]), ALU.subtract).then_inc(enc_low, 1)
                if step == "max":
                    for i in range(2):
                        dve.wait_ge(cmax_ready, 2 * n1 + i + 1)
                        nc.vector.tensor_reduce(lane.crow_max[:, 2 * i:2 * i + 2],
                                                banks[i][:, :].rearrange("p (s m) -> p s m", s=2),
                                                AX.X, ALU.max).then_inc(crow_max_ready, 1)
                if step == "normalize":
                    turned = banks[0][:, 0:SUBS * (LATENT + 1)].rearrange("p (s c) -> p s c", s=SUBS)
                    dve.wait_ge(csums_turned, n1 + 1)
                    nc.vector.reciprocal(lane.cinv[:, :], turned[:, :, LATENT]).then_inc(cinv_ready, 1)
                    dve.wait_ge(cinv_ready, n1 + 1)
                    dve.wait_ge(lane.clat_stored, 16 * had + FIRST)
                    nc.vector.tensor_tensor(lane.clat_out[:, :, :], turned[:, :, 0:LATENT],
                                            lane.cinv[:, :].unsqueeze(2).to_broadcast([PART, SUBS, LATENT]),
                                            ALU.mult).then_inc(clat_ready, 1)

            def output_step(k, n2, had, lane=lanes[0], banks=side_bank):
                if k == 0:
                    dve.wait_ge(lane.resid_loaded, 16 * (had + 1))
                dve.wait_ge(resid_ready, KTILES * n2 + k + 1)
                nc.vector.tensor_tensor(lane.resid[:, k, :], lane.resid[:, k, :], banks[1 - k % 2][:, :],
                                        ALU.add).then_inc(resid_added, 1)

            def attend(b, j, parity, side, first=False, last=False):
                n = b * BLOCKS + j
                if first:
                    first_search(b, BLOCKS - 1)
                    finish_max(n)
                    low_values(b, BLOCKS - 1)
                done = 0
                for t in range(KEYTILES):
                    add_probs(b, j, t)
                    if not last:
                        for i in range(done, SEARCHED[t]):
                            take_max((n + 1) * SEARCHES + i, tile_max[:, i % SUBS, i // SUBS:i // SUBS + 1],
                                     max_bank[i % 2])
                        if done < SEARCHES == SEARCHED[t]:
                            finish_max(n + 1)
                        done = SEARCHED[t]
                    if t == DVE_TURN and not first:
                        normalize(b, j - 1)
                    if side >= 1 and t in DVE_CONCEPT:
                        concept_step(DVE_CONCEPT[t], n - BLOCKS, n - BLOCKS)
                    if side >= 2 and t in DVE_OUTPUT:
                        output_step(DVE_OUTPUT[t], n - 2 * BLOCKS, n - 2 * BLOCKS)

            def tail(pair, concept):
                blocks = list(tail_blocks(pair, concept))

                def concept_steps(step):
                    for i, (lane, j, n1, n2, had1, had2) in enumerate(blocks):
                        concept_step(step, n1, had1, lane, tail_banks[i])

                if concept:
                    concept_steps("enc")
                    concept_steps("max")
                for i, (lane, j, n1, n2, had1, had2) in enumerate(blocks):
                    for k in range(KTILES):
                        output_step(k, n2, had2, lane, tail_out_banks[i])
                if concept:
                    concept_steps("normalize")

            def finish(b):
                normalize(b, BLOCKS - 1)
                if is_last(b):
                    nc.vector.memset(raw(lanes[1].cqueries_shift[64:128, :]), 0.0)

            schedule(dve.Fori, project, attend, finish, tail)

        @block.tensor
        def _(pe):
            mm = nc.tensor.matmul
            pe.wait_ge(setup_dve, SETUP_STEPS)
            for k in range(KTILES):
                last = mm(side_bank[0][0:64, 0:LATENT], raw_o[:, k, :], raw_tp[:, k, 0:LATENT],
                          start=k == 0, stop=k == KTILES - 1)
            last.then_inc(setup_pe, 1)
            pe.wait_ge(setup_ready, 1)

            def first_search(b, j, s):
                entry = b * BLOCKS * SEARCHES + j * SUBS + s
                pe.wait_ge(high_ready, b * BLOCKS + j + 1)
                pe.wait_ge(max_taken, entry + 1)
                mm(first_search_bank[s][:, :], search_q[:, 0, s * PART:(s + 1) * PART], keys_high[:, block_cols(j)],
                   start=True, stop=True).then_inc(max_ready, 1)

            def search(kb, parity, i):
                entry = kb * SEARCHES + i
                pe.wait_ge(max_taken, entry - 1 + SEARCH_BANKS)
                mm(max_bank[i % 2][:, :], search_q[:, parity, (i % SUBS) * PART:(i % SUBS + 1) * PART],
                   keys_high[:, (i // SUBS) * BLOCK:(i // SUBS + 1) * BLOCK], start=True, stop=True)\
                    .then_inc(max_ready, 1)

            def shift_row(kb):
                pe.wait_ge(row_max_ready, kb + 1)
                for s in range(SUBS):
                    last = mm(max_bank[0][0:1, s * PART:(s + 1) * PART], row_max[:, s:s + 1], neg_ident[:, :],
                              start=True, stop=True)
                last.then_inc(shift_ready, 1)

            def turn_g(b, j):
                kb = b * BLOCKS + j
                pe.wait_ge(g_copied, kb + 1)
                pe.wait_ge(values_ready, kb + FIRST)
                for s in range(SUBS):
                    last = mm(side_bank[1][:, s * LATENT:(s + 1) * LATENT], g_parts[:, s * PART:(s + 1) * PART],
                              fold[:, :], start=True, stop=True)
                last.then_inc(g_turned, 1)

            def project(b, j, parity):
                kb = b * BLOCKS + j
                first = isinstance(j, int) and j == 0
                tp, g = score_bank[parity], side_bank[0]
                high = x_high[:, parity, :, :]

                def product(out, weights, part, start=False, stop=False):
                    for k in range(KTILES):
                        last = mm(out[:, :], weights[:, k, :], part[:, k, :],
                                  start=start and k == 0, stop=stop and k == KTILES - 1)
                    return last

                pe.wait_ge(x_high_ready, kb + 1)
                pe.wait_ge(low_ready, kb - 1 + FIRST)
                product(tp, w_tp_high, high, start=True)
                product(tp, w_tp_low, high)
                if first and not (isinstance(b, int) and b == 0):
                    finish(b - 1)
                if first:
                    pe.wait_ge(lat_ready, b * BLOCKS + FIRST)
                    if not isinstance(b, int) or b > 1:
                        pe.wait_ge(clat_ready, (b - 1) * BLOCKS + FIRST)
                else:
                    pe.wait_ge(search_q_loaded[0], 16 * (b * (BLOCKS // 2) + 1))
                    first_search(b, j - 1, 0)
                if not (isinstance(kb, int) and kb == 0):
                    pe.wait_ge(g_copied, kb)
                product(g, w_g_split, high, start=True)
                if not first:
                    first_search(b, j - 1, 1)
                    turn_g(b, j - 1)
                pe.wait_ge(x_low_pool, kb + 1)
                pe.wait_ge(x_low_dve, kb + 1)
                product(tp, w_tp_high, x_low, stop=True).then_inc(thetaphi_ready, 1)
                if not first:
                    first_search(b, j - 1, 2)
                product(g, w_g_split, x_low, stop=True).then_inc(g_ready, 1)
                if not first:
                    first_search(b, j - 1, 3)

            def score(b, j, t):
                mm(score_bank[t % 2][:, :], keys_high[:, t * PART:(t + 1) * PART], queries_flat[:, q_cols(b, j)],
                   start=True, stop=False)
                mm(score_bank[t % 2][:, :], keys_low[:, t * PART:(t + 1) * PART], queries_shift[:, block_cols(j)],
                   start=False, stop=True).then_inc(scores_ready, 1)

            def turn(b, j, s):
                kb = b * BLOCKS + j
                if s == 0:
                    pe.wait_ge(sums_copied, kb + 1 + FIRST)
                    pe.wait_ge(probs_added, (kb + 1) * KEYTILES)
                    pe.wait_ge(lat_ready, kb + FIRST)
                at = s * (LATENT + 1)
                mm(side_bank[1][:, at:at + LATENT], sums_t[:, s * PART:(s + 1) * PART], fold[:, :],
                   start=True, stop=True)
                last = mm(side_bank[1][:, at + LATENT:at + LATENT + 1], total[:, s * PART:(s + 1) * PART],
                          ones[:, :], start=True, stop=True)
                if s == SUBS - 1:
                    last.then_inc(sums_turned, 1)

            def concept_step(step, b1, j, lane=lanes[0], banks=side_bank):
                n1 = b1 * BLOCKS + j
                if step == "enc":
                    pe.wait_ge(lat_low, n1 + 1 + FIRST)
                    mm(banks[0][0:64, :], w_to_high[:, :], lane.lat_split[:, :], start=True, stop=False)
                    mm(banks[0][0:64, :], w_to_low[:, :], lane.lat_split[:, :], start=False, stop=False)
                    mm(banks[0][0:64, :], fold_r[:, :], queries_flat[:, q_cols(b1, j)],
                       start=False, stop=True).then_inc(enc_ready, 1)
                if step == "max":
                    pe.wait_ge(enc_low, n1 + 1)
                    for i in range(2):
                        for h in range(2):
                            s = 2 * i + h
                            last = mm(banks[i][:, h * CONCEPTS:(h + 1) * CONCEPTS],
                                      lane.cqueries[:, s * PART:(s + 1) * PART], ckeys_high[:, :],
                                      start=True, stop=True)
                        last.then_inc(cmax_ready, 1)
                if step == "shift":
                    pe.wait_ge(crow_max_ready, 2 * (n1 + 1))
                    for s in range(SUBS):
                        last = mm(banks[0][0:1, s * PART:(s + 1) * PART], lane.crow_max[:, s:s + 1],
                                  neg_ident[:, :], start=True, stop=True)
                    last.then_inc(cshift_ready, 1)
                if step in ("scores 0", "scores 1"):
                    t = int(step[-1])
                    pe.wait_ge(cshift_taken, n1 + 1)
                    mm(banks[1 - t][:, :], ckeys_high[:, t * PART:(t + 1) * PART], lane.cqueries[:, :],
                       start=True, stop=False)
                    mm(banks[1 - t][:, :], ckeys_low[:, t * PART:(t + 1) * PART], lane.cqueries_shift[:, :],
                       start=False, stop=True).then_inc(cscores_ready, 1)
                if step in ("sums 0", "sums 1"):
                    t = int(step[-1])
                    pe.wait_ge(cprobs_ready, CTILES * (n1 + 1))
                    mm(banks[1][0:LATENT + 1, :], cvalues[:, t, :], lane.cprobs[:, t, :],
                       start=t == 0, stop=t == CTILES - 1).then_inc(csums_ready, 1)
                if step == "turn":
                    pe.wait_ge(csums_copied, n1 + 1)
                    for s in range(SUBS):
                        last = nc.tensor.transpose(banks[0][:, s * (LATENT + 1):(s + 1) * (LATENT + 1)],
                                                   lane.csums_t[:, s * PART:(s + 1) * PART],
                                                   ident[0:LATENT + 1, 0:LATENT + 1])
                    last.then_inc(csums_turned, 1)

            def output_step(k, n2, lane=lanes[0], banks=side_bank):
                if k == 0:
                    pe.wait_ge(mix_low, n2 + 1 + FIRST)
                if k >= 2:
                    pe.wait_ge(resid_added, KTILES * n2 + k - 1 + FIRST)
                mm(banks[1 - k % 2][:, :], w_ot_high[:, k * PART:(k + 1) * PART], lane.mix_split[:, :],
                   start=True, stop=False)
                mm(banks[1 - k % 2][:, :], w_ot_low[:, k * PART:(k + 1) * PART], lane.mix_split[:, :],
                   start=False, stop=True).then_inc(resid_ready, 1)

            def attend(b, j, parity, side, first=False, last=False):
                kb = b * BLOCKS + j
                if first:
                    for s in range(SUBS):
                        first_search(b, BLOCKS - 1, s)
                    turn_g(b, BLOCKS - 1)
                    shift_row(kb)
                    pe.wait_ge(low_ready, (b + 1) * BLOCKS + FIRST)
                    pe.wait_ge(shift_taken, kb + 1)
                    pe.wait_ge(values_ready, (b + 1) * BLOCKS + FIRST)
                    for t in range(LEAD):
                        if t >= 2:
                            pe.wait_ge(probs_high_ready, kb * KEYTILES + t - 1)
                        score(b, 0, t)
                done = 0
                for t in range(KEYTILES):
                    n = kb * KEYTILES + t
                    if not last:
                        if t == 0:
                            pe.wait_ge(search_q_loaded[1 - parity], 16 * (b * (BLOCKS // 2) + (j + 1) // 2 + 1))
                        if done < SEARCHED[t]:
                            search(kb + 1, 1 - parity, done)
                        if t == SHIFT_STEP:
                            shift_row(kb + 1)
                    ahead = t + LEAD
                    if ahead < KEYTILES or not last:
                        if ahead == KEYTILES:
                            pe.wait_ge(shift_taken, kb + 2)
                        pe.wait_ge(probs_high_ready, n + LEAD - 1)
                        if ahead < KEYTILES:
                            score(b, j, ahead)
                        else:
                            score(b, j + 1, ahead - KEYTILES)
                    if t == 0:
                        pe.wait_ge(sums_copied, kb + FIRST)
                    pe.wait_ge(probs_high_ready, n + 1)
                    mm(sum_bank[:, :], values[:, t, :], probs_high[:, t % NE, :], start=t == 0, stop=False)
                    if not last:
                        for i in range(done + 1, SEARCHED[t]):
                            search(kb + 1, 1 - parity, i)
                        done = SEARCHED[t]
                    pe.wait_ge(probs_low_ready, n + 1)
                    mm(sum_bank[:, :], values[:, t, :], probs_low[:, t % NL, :],
                       start=False, stop=t == KEYTILES - 1).then_inc(probs_used, 1)
                    if t in PE_TURN and not first:
                        if side >= 2 and PE_TURN[t] == 0:
                            pe.wait_ge(resid_added, KTILES * (kb - 2 * BLOCKS) + FIRST)
                        turn(b, j - 1, PE_TURN[t])
                    if side >= 1 and t in PE_CONCEPT:
                        if PE_CONCEPT[t] == "enc":
                            pe.wait_ge(clat_ready, kb - BLOCKS + FIRST)
                            if side >= 2:
                                pe.wait_ge(resid_added, KTILES * (kb - 2 * BLOCKS) + FIRST)
                        if PE_CONCEPT[t] == "max":
                            pe.wait_ge(lat_ready, kb + FIRST)
                        concept_step(PE_CONCEPT[t], b - 1, j)
                    if side >= 2 and t in PE_OUTPUT:
                        if PE_OUTPUT[t] == 1:
                            pe.wait_ge(clat_ready, kb - BLOCKS + 1 + FIRST)
                        output_step(PE_OUTPUT[t], kb - 2 * BLOCKS)

            def finish(b):
                if not isinstance(b, int) or b > 1:
                    pe.wait_ge(resid_added, KTILES * BLOCKS * (b - 1) + FIRST)
                for s in range(SUBS):
                    turn(b, BLOCKS - 1, s)

            def tail(pair, concept):
                blocks = list(tail_blocks(pair, concept))

                def concept_steps(*steps):
                    for i, (lane, j, n1, n2, had1, had2) in enumerate(blocks):
                        for step in steps:
                            concept_step(step, BATCH - 1, j, lane, tail_banks[i])

                def output_steps(i):
                    lane, j, n1, n2, had1, had2 = blocks[i]
                    for k in range(KTILES):
                        output_step(k, n2, lane, tail_out_banks[i])

                pe.wait_ge(resid_added, KTILES * blocks[0][3] + FIRST)
                if concept:
                    pe.wait_ge(lat_ready, BATCH * BLOCKS + FIRST)
                    pe.wait_ge(clat_ready, blocks[0][2] + FIRST)
                    concept_steps("enc")
                    concept_steps("max")
                output_steps(0)
                if concept:
                    concept_steps("shift")
                output_steps(1)
                if concept:
                    concept_steps("scores 0", "scores 1")
                    concept_steps("sums 0", "sums 1")
                    concept_steps("turn")

            schedule(pe.Fori, project, attend, finish, tail)


DVE_TURN = 6
PE_TURN = {2: 0, 3: 1, 4: 2, 5: 3}
PE_CONCEPT = {8: "enc", 12: "max", 15: "shift", 18: "scores 0", 19: "scores 1", 21: "sums 0", 22: "sums 1",
              25: "turn"}
ACT_CONCEPT = {4: "lat", 11: "enc", 18: "shift", 22: "probs", 25: "sums"}
DVE_CONCEPT = {10: "enc", 13: "max", 25: "normalize"}
POOL_CONCEPT = 5
PE_OUTPUT = {26: 0, 27: 1, 29: 2, 30: 3}
POOL_OUTPUT = {"mix": 12, "low": 18}
ACT_OUTPUT = 16
DVE_OUTPUT = {27: 0, 29: 1, 30: 2, 31: 3}


def kernel(x, L0_conv_concepts, L0_conv_w_theta, L0_conv_w_phi, L0_conv_w_g, L0_conv_w_o,
           L0_conv_gamma_sa, L0_conv_gamma_moca):
    import numpy as np
    import concourse.bacc as bacc
    from concourse import mybir
    from concourse.bass_utils import run_bass_kernel_spmd

    def by_partition(a):
        return np.ascontiguousarray(a.reshape(-1, PART, a.shape[1]).transpose(1, 0, 2))

    x = np.ascontiguousarray(x)
    theta, phi, g, w_o = (np.asarray(a) for a in (L0_conv_w_theta, L0_conv_w_phi, L0_conv_w_g, L0_conv_w_o))
    concepts = np.asarray(L0_conv_concepts)
    arrays = {
        "x": x.reshape(BATCH, CH, PIXELS),
        "w_thetaphi": by_partition(np.concatenate([theta, phi], axis=0).T),
        "w_g": by_partition(g.T),
        "w_o_t": np.ascontiguousarray(w_o.T),
        "w_o": by_partition(w_o),
        "concepts_t": np.ascontiguousarray(concepts.T),
        "concepts": by_partition(concepts),
        "gamma_sa": np.asarray(L0_conv_gamma_sa).reshape(1),
        "gamma_moca": np.asarray(L0_conv_gamma_moca).reshape(1),
        "consts": np.eye(PART, dtype=np.float32),
    }
    nc = bacc.Bacc("TRN2", target_bir_lowering=False, num_devices=1)
    args = {n: nc.dram_tensor(f"in_{n}", a.shape, mybir.dt.from_np(a.dtype), kind="ExternalInput").ap()
            for n, a in arrays.items()}
    out = nc.dram_tensor("out_0", (BATCH, CH, PIXELS), mybir.dt.float32, kind="ExternalOutput").ap()
    attention_kernel(nc, out=out, **args)
    r = run_bass_kernel_spmd(nc, [{f"in_{n}": a for n, a in arrays.items()}], core_ids=[0])
    return r.results[0]["out_0"].reshape(x.shape)
```
